# Optimizing a Trainium2 kernel written in Bass

```python
import numpy as np
import jax
import jax.numpy as jnp

def _softmax(x, axis=-1):
    return jax.nn.softmax(x, axis=axis)

def _gelu(x):
    return jax.nn.gelu(x, approximate=True)

def _silu(x):
    return jax.nn.silu(x)

def _sigmoid(x):
    return jax.nn.sigmoid(x)

def _layernorm(x, axis=-1, eps=1e-05):
    m = jnp.mean(x, axis=axis, keepdims=True)
    v = jnp.var(x, axis=axis, keepdims=True)
    return (x - m) / jnp.sqrt(v + eps)

def _scatter_add(tgt, idx, src, axis=0):
    return tgt.at[idx].add(src)

def _segment_sum(src, seg, n):
    return jax.ops.segment_sum(src, seg, n)
kernel_name = 'mk_flamingo_gated_d1_seqx_r8_857fcb'

def setup_inputs(seed: int=0):
    np.random.seed(seed)
    _w = jnp.asarray

    def _rec_inputs():
        import jax
        import jax.numpy as jnp
        _rk = jax.random.key(seed)
        x = -0.0002928 + 1 * jax.random.normal(jax.random.fold_in(_rk, 1), (64, 128, 128), jnp.float32)
        _lenS = 128 - jax.random.randint(jax.random.fold_in(_rk, 7), (64,), 0, max(1, 128 // 4) + 1, jnp.int32)
        _lenS2 = 77 - jax.random.randint(jax.random.fold_in(_rk, 8), (64,), 0, max(1, 77 // 4) + 1, jnp.int32)
        _ctx_1024P = jax.random.normal(jax.random.fold_in(_rk, 11), (64, 16, 128), jnp.float32)
        _ctx_1024c = jax.random.dirichlet(jax.random.fold_in(_rk, 511), 0.3 * jnp.ones((16,), jnp.float32), (64, 77))
        _ctx_1024t = jnp.einsum('bsk,bkd->bsd', _ctx_1024c, _ctx_1024P)
        _ctx_1024t = _ctx_1024t * jax.lax.rsqrt(jnp.mean(jnp.square(_ctx_1024t)) + 1e-12) * 0.953939
        ctx_1024 = -1.39393e-06 + 0.999914 * (_ctx_1024t + 0.3 * jax.random.normal(jax.random.fold_in(_rk, 611), (64, 77, 128), jnp.float32))
        fside_BxSxS2_0 = jax.random.uniform(jax.random.fold_in(_rk, 12), (64, 128, 77), jnp.float32, 0.0, 1)
        _validS = jnp.arange(128)[None, :] < _lenS[:, None]
        _validS2 = jnp.arange(77)[None, :] < _lenS2[:, None]
        _causal = jnp.tril(jnp.ones((128, 128), dtype=bool))
        mask_BxSxS2_ik1 = jnp.where(jnp.broadcast_to(_validS2[:, None, :], (64, 128, 77)), 1, 0).astype(jnp.int32)
        _g = jax.random.normal(jax.random.fold_in(_rk, 9001), (2, 1), jnp.float32)
        _g = jnp.sign(_g) * jnp.maximum(jnp.abs(_g), 1.0) + (_g == 0) * 1.0
        g_xattn = _g[0]
        g_ffn = _g[1]
        return (x, ctx_1024, fside_BxSxS2_0, mask_BxSxS2_ik1, g_xattn, g_ffn)
    x, ctx_1024, fside_BxSxS2_0, mask_BxSxS2_ik1, g_xattn, g_ffn = _rec_inputs()

    def _L0_xattn_setup():
        import jax, jax.numpy as jnp
        import numpy as np
        NUM_HEADS = 16
        HIDDEN = 128
        B, S = (2, 256)

        def _split_heads(x, H):
            b, s, d = x.shape
            return x.reshape(b, s, H, d // H).transpose(0, 2, 1, 3)
        key = jax.random.key(seed)
        ks = jax.random.split(key, 14)
        D = HIDDEN
        scale = 1.0 / np.sqrt(D)
        inp = {'query': jax.random.normal(ks[0], (B, S, D), jnp.float32), 'key_in': jax.random.normal(ks[1], (B, S, D), jnp.float32), 'value': jax.random.normal(ks[2], (B, S, D), jnp.float32), 'group_prob': jax.random.uniform(ks[3], (B, S, S), jnp.float32), 'mask': jax.random.randint(ks[4], (B, S, S), 0, 2, jnp.int32), 'wq_k': jax.random.normal(ks[5], (D, D), jnp.float32) * scale, 'wq_b': jnp.zeros((D,), jnp.float32), 'wk_k': jax.random.normal(ks[6], (D, D), jnp.float32) * scale, 'wk_b': jnp.zeros((D,), jnp.float32), 'wv_k': jax.random.normal(ks[7], (D, D), jnp.float32) * scale, 'wv_b': jnp.zeros((D,), jnp.float32), 'wo_k': jax.random.normal(ks[8], (D, D), jnp.float32) * scale, 'wo_b': jnp.zeros((D,), jnp.float32)}
        return inp
    _L0_xattn_all = _L0_xattn_setup()
    _L0_xattn_in = {k: v for k, v in _L0_xattn_all.items() if k in ('wq_k', 'wq_b', 'wk_k', 'wk_b', 'wv_k', 'wv_b', 'wo_k', 'wo_b')}
    del _L0_xattn_all

    def _L0_ffn_setup():
        import jax, jax.numpy as jnp
        import numpy as np
        DMODEL = 128
        N_EXPERTS = 32
        EXPERT_SIZE = 64
        N_HEADS = 4
        WEIGHT_SCALE = 1.0
        key = jax.random.key(seed)
        k0, k1, k2, k3 = jax.random.split(key, 4)
        x = jax.random.normal(k0, (2, 256, DMODEL), dtype=jnp.float32)
        expert_sel = jax.random.normal(k1, (N_EXPERTS, DMODEL), dtype=jnp.float32) * DMODEL ** (-0.5)
        keys = jax.random.normal(k2, (N_EXPERTS, DMODEL, EXPERT_SIZE), dtype=jnp.float32) * DMODEL ** (-0.5)
        values = jax.random.normal(k3, (N_EXPERTS, EXPERT_SIZE, DMODEL), dtype=jnp.float32) * (N_EXPERTS * EXPERT_SIZE) ** (-0.5)
        return {'x': x, 'expert_sel': expert_sel, 'keys': keys, 'values': values}
    _L0_ffn_all = _L0_ffn_setup()
    _L0_ffn_in = {k: v for k, v in _L0_ffn_all.items() if k in ('expert_sel', 'keys', 'values')}
    del _L0_ffn_all
    return {'x': x, 'ctx_1024': ctx_1024, 'fside_BxSxS2_0': fside_BxSxS2_0, 'mask_BxSxS2_ik1': mask_BxSxS2_ik1, 'g_xattn': g_xattn, 'g_ffn': g_ffn, 'L0_xattn_wq_k': _L0_xattn_in['wq_k'], 'L0_xattn_wq_b': _L0_xattn_in['wq_b'], 'L0_xattn_wk_k': _L0_xattn_in['wk_k'], 'L0_xattn_wk_b': _L0_xattn_in['wk_b'], 'L0_xattn_wv_k': _L0_xattn_in['wv_k'], 'L0_xattn_wv_b': _L0_xattn_in['wv_b'], 'L0_xattn_wo_k': _L0_xattn_in['wo_k'], 'L0_xattn_wo_b': _L0_xattn_in['wo_b'], 'L0_ffn_expert_sel': _L0_ffn_in['expert_sel'], 'L0_ffn_keys': _L0_ffn_in['keys'], 'L0_ffn_values': _L0_ffn_in['values']}

def reference(x, ctx_1024, fside_BxSxS2_0, mask_BxSxS2_ik1, g_xattn, g_ffn, L0_xattn_wq_k, L0_xattn_wq_b, L0_xattn_wk_k, L0_xattn_wk_b, L0_xattn_wv_k, L0_xattn_wv_b, L0_xattn_wo_k, L0_xattn_wo_b, L0_ffn_expert_sel, L0_ffn_keys, L0_ffn_values):
    import jax
    import jax.numpy as jnp

    def _L0_xattn_ref(query, key_in, value, group_prob, mask, wq_k, wq_b, wk_k, wk_b, wv_k, wv_b, wo_k, wo_b):
        import jax, jax.numpy as jnp
        import numpy as np
        NUM_HEADS = 16
        HIDDEN = 128
        B, S = (2, 256)

        def _split_heads(x, H):
            b, s, d = x.shape
            return x.reshape(b, s, H, d // H).transpose(0, 2, 1, 3)
        H = NUM_HEADS
        dh = query.shape[-1] // H
        q = _split_heads(query @ wq_k + wq_b, H)
        k = _split_heads(key_in @ wk_k + wk_b, H)
        v = _split_heads(value @ wv_k + wv_b, H)
        logits = jnp.einsum('bhqd,bhkd->bhqk', q, k) / jnp.sqrt(jnp.asarray(dh, q.dtype))
        neg = (1.0 - mask.astype(q.dtype)) * -1000000000.0
        logits = logits + neg[:, None, :, :]
        attn = jax.nn.softmax(logits, axis=-1)
        attn = attn * group_prob[:, None, :, :]
        out = jnp.einsum('bhqk,bhkd->bhqd', attn, v)
        out = out.transpose(0, 2, 1, 3).reshape(query.shape[0], -1, H * dh)
        return out @ wo_k + wo_b

    def _L0_ffn_ref(x, expert_sel, keys, values):
        import jax, jax.numpy as jnp
        import numpy as np
        DMODEL = 128
        N_EXPERTS = 32
        EXPERT_SIZE = 64
        N_HEADS = 4
        WEIGHT_SCALE = 1.0
        B, S, D = x.shape
        xt = x.reshape(-1, D)
        N = xt.shape[0]
        sel_logits = jnp.einsum('nd,ed->ne', xt, expert_sel)
        gates = jax.nn.sigmoid(sel_logits)
        sel_val, sel_idx = jax.lax.top_k(gates, N_HEADS)
        gate_full = jnp.zeros_like(gates).at[jnp.arange(N)[:, None], sel_idx].set(sel_val)
        scores = jax.nn.relu(jnp.einsum('nd,edf->nef', xt, keys))
        scores = scores * gate_full[:, :, None]
        out = jnp.einsum('nef,efv->nv', scores, values)
        return out.reshape(B, S, -1)
    x = x + jnp.tanh(g_xattn[0]) * _L0_xattn_ref(_layernorm(x, axis=-1), ctx_1024, ctx_1024, fside_BxSxS2_0, mask_BxSxS2_ik1, L0_xattn_wq_k, L0_xattn_wq_b, L0_xattn_wk_k, L0_xattn_wk_b, L0_xattn_wv_k, L0_xattn_wv_b, L0_xattn_wo_k, L0_xattn_wo_b)
    x = x + jnp.tanh(g_ffn[0]) * _L0_ffn_ref(_layernorm(x, axis=-1), L0_ffn_expert_sel, L0_ffn_keys, L0_ffn_values)
    return x

_drawn_inputs = setup_inputs


def setup_inputs(seed=0):
    import zlib

    import numpy as np

    out = dict(_drawn_inputs(seed))
    spreads = {'L0_xattn_wq_b': (0.0, 0.345),
     'L0_xattn_wk_b': (0.0, 0.8),
     'L0_xattn_wv_b': (0.0, 0.1),
     'L0_xattn_wo_b': (0.0, 0.1)}
    factors = {}
    for name, (base, spread) in spreads.items():
        noise = np.random.default_rng([zlib.crc32(name.encode()), seed]).standard_normal(out[name].shape)
        drawn = base * np.exp(spread * noise) if base else spread * noise
        out[name] = jnp.asarray(drawn.astype(out[name].dtype))
    for name, factor in factors.items():
        out[name] = (out[name] * factor).astype(out[name].dtype)
    return out
```

```python
from contextlib import ExitStack

import numpy as np
import concourse.bass as bass
from concourse import mybir

F32 = mybir.dt.float32
F16 = mybir.dt.float16
BF16 = mybir.dt.bfloat16
I32 = mybir.dt.int32
ALU = mybir.AluOpType
ACT = mybir.ActivationFunctionType
AX = mybir.AxisListType
ABSMAX = bass.bass_isa.ReduceOp.absmax

P = 128
B, S, D = 64, 128, 128
KEYS = 77
H, DH = 16, 8
QUADS = 4
KMAIN = 64
KREM = KEYS - KMAIN
HALF = H // 2
EXPERTS, FE, TOP = 32, 64, 4
BLOCKS = EXPERTS * FE // P
TILES = 4
GROUPS = B // TILES
GT = TILES * P
UNROLL = 4
LAG = 4
X_CUTS = [0, 8, 36, 64]
MAIN_STEP = P + 2 * DH
REM_STEP = P + HALF * DH
EPS = 1e-5
HIDDEN_SHIFT = 2.0 ** -5
SCALED_EXP = 12
LEAST_EXP = 20
EXP_MASK = 0x7F800000

CHUNKS = [("rem", 0), ("main", 0), ("main", 1), ("main", 2),
          ("main", 3), ("rem", 1), ("main", 4), ("main", 5),
          ("main", 6), ("main", 7)]
SETS = [CHUNKS[0:4], CHUNKS[4:8], CHUNKS[8:10]]


def build(nc, x, ctx_in, fside, mask, g_xattn, g_ffn, wq, bq, wk, bk, wv, bv, wo, bo,
          expert_sel, keys, values, ident_c, headmask_c, remmask_c, gatesel_c, restart_c, out):
    with ExitStack() as stack:
        def sb(name, shape, dt=F32):
            return stack.enter_context(nc.sbuf_tensor(name, shape, dt))

        def sem(name):
            return stack.enter_context(nc.semaphore(name))

        def sems(name, n):
            return [sem(f"{name}{i}") for i in range(n)]

        ps = stack.enter_context(nc.psum_tensor("ps", [P, 8, 512], F32))
        bank_ct, bank_proj, bank_lg, bank_pt, bank_o = 0, 1, (2, 3), (4, 5, 6), 7
        bank_sg, bank_xy, bank_u, bank_g, bank_y = 0, 1, (2, 3), (4, 5), (6, 7)

        ident = sb("ident", [P, P])
        identb = sb("identb", [P, P], BF16)
        headmask = sb("headmask", [P, 4])
        remmask = sb("remmask", [P, P])
        gatesel = sb("gatesel", [96, EXPERTS, FE], BF16)
        restart = sb("restart", [P, P])
        wq_sb, wk_sb, wv_sb, wo_sb = (sb(n, [P, P]) for n in ("wq_sb", "wk_sb", "wv_sb", "wo_sb"))
        wo_g = sb("wo_g", [P, P])
        bias_q, bias_k, bias_qs = sb("bias_q", [P, 1]), sb("bias_k", [P, 1]), sb("bias_qs", [P, 1])
        bv_rows, bo_rows = sb("bv_rows", [P, P]), sb("bo_rows", [P, P])
        bv_rem, bo_g = sb("bv_rem", [P, P]), sb("bo_g", [P, P])
        gates_in, gates_tanh = sb("gates_in", [P, 2]), sb("gates_tanh", [P, 2])
        gatesel_f = sb("gatesel_f", [96, EXPERTS])
        keys_raw = sb("keys_raw", [P, EXPERTS * FE])
        values_raw = sb("values_raw", [P, BLOCKS * P])
        keys_hi, keys_lo = sb("keys_hi", [P, EXPERTS * FE], F16), sb("keys_lo", [P, EXPERTS * FE], F16)
        values_hi, values_lo = sb("values_hi", [P, BLOCKS * P], F16), sb("values_lo", [P, BLOCKS * P], F16)
        selT = sb("selT", [P, EXPERTS])
        sel_hi, sel_lo = sb("sel_hi", [P, EXPERTS], F16), sb("sel_lo", [P, EXPERTS], F16)
        magn, magn_all = sb("magn", [P, 3]), sb("magn_all", [P, 3])
        magn_exp = sb("magn_exp", [P, 3], I32)
        scaled = sb("scaled", [P, 2, P])
        scale_w, unscale_w = sb("scale_w", [P, 3]), sb("unscale_w", [P, 3])
        neg_unscale_sel, y_scale = sb("neg_unscale_sel", [P, 1]), sb("y_scale", [P, 2])

        x_all = sb("x_all", [P, B, D])
        bn1, bn2 = sb("bn1", [P, B, 6]), sb("bn2", [P, B, 6])
        mean1, mean2 = sb("mean1", [P, B]), sb("mean2", [P, B])
        rstd1, rstd2 = sb("rstd1", [P, B]), sb("rstd2", [P, B])
        norm_tmp = sb("norm_tmp", [P, 8, B])

        ctx_main, ctx_rem = sb("ctx_main", [P, 2, D]), sb("ctx_rem", [P, 2, D])
        prob_g = sb("prob_g", [P, 2, KEYS])
        mask_in = sb("mask_in", [P, 2, KEYS], I32)
        negm = sb("negm", [P, 2, KEYS])
        xn = sb("xn", [P, 2, D])
        ct = sb("ct", [P, 2, 4 * P])
        qT = sb("qT", [P, 2, P])
        kv = sb("kv", [P, 2, KEYS + 2 * P])
        kblk = sb("kblk", [P, 2, 4, KEYS])
        vmain = sb("vmain", [P, 2, HALF * MAIN_STEP])
        vrem_m, vrem = sb("vrem_m", [P, 2, P]), sb("vrem", [P, 2, 2 * REM_STEP])
        soft = sb("soft", [P, 2, H, KEYS])
        negmax, sums = sb("negmax", [P, 2, H]), sb("sums", [P, 2, H])
        rsum = sb("rsum", [P, 2, H])
        wmain, wrem = sb("wmain", [P, 2, H, KMAIN]), sb("wrem", [P, 2, 2, P])
        wT = sb("wT", [P, 2, len(CHUNKS), P])
        rexp = sb("rexp", [P, H, DH])
        oT = sb("oT", [P, P])
        xb = sb("xb", [P, 2, D])

        x2 = sb("x2", [P, TILES, D])
        x2_hi, x2_lo = sb("x2_hi", [P, 2, GT], F16), sb("x2_lo", [P, 2, GT], F16)
        egate, gate = sb("egate", [P, TILES, EXPERTS]), sb("gate", [P, TILES, EXPERTS])
        dgate = sb("dgate", [P, TILES, EXPERTS])
        best = sb("best", [P, TILES, 8])
        above, equal = sb("above", [P, TILES, EXPERTS]), sb("equal", [P, TILES, EXPERTS])
        n_above, rank = sb("n_above", [P, TILES]), sb("rank", [P, TILES, EXPERTS])
        rank2, taken = sb("rank2", [P, TILES, EXPERTS]), sb("taken", [P, TILES, EXPERTS])
        kept, gsel = sb("kept", [P, TILES, EXPERTS]), sb("gsel", [P, TILES, EXPERTS])
        grest1, grest2 = sb("grest1", [P, TILES, EXPERTS]), sb("grest2", [P, TILES, EXPERTS])
        gparts = sb("gparts", [P, TILES, 3, EXPERTS], BF16)
        gT = sb("gT", [96, 2, GT], BF16)
        relu_u = sb("relu_u", [P, 2, GT])
        hid = sb("hid", [P, LAG, GT])
        hid_hi, hid_lo = sb("hid_hi", [P, LAG, GT], F16), sb("hid_lo", [P, LAG, GT], F16)
        yT, y_out = sb("yT", [P, GT]), sb("y_out", [P, 2, TILES, D])

        weights_in, small_in = sem("weights_in"), sem("small_in")
        x_in = sems("x_in", len(X_CUTS) - 1)
        experts_in = sem("experts_in")
        zeroed, tanh_done, gated_w = sem("zeroed"), sem("tanh_done"), sem("gated_w")
        bn1_ready = sem("bn1_ready")
        ctx_ld, g_ld, mask_ld = sems("ctx_ld", 2), sems("g_ld", 2), sems("mask_ld", 2)
        negm_ready, xn_ready = sem("negm_ready"), sem("xn_ready")
        ct_done, ct_copied, proj_done = sem("ct_done"), sem("ct_copied"), sem("proj_done")
        q_ready, k_copied, v_copied = sem("q_ready"), sem("k_copied"), sem("v_copied")
        kblk_ready, vmain_ready = sem("kblk_ready"), sem("vmain_ready")
        vremm_ready, vrem_ready = sem("vremm_ready"), sem("vrem_ready")
        lg_done, lg_masked = sems("lg_done", QUADS), sems("lg_masked", QUADS)
        max_ready = sems("max_ready", 2)
        shifted, exp_done = sem("shifted"), sems("exp_done", 2)
        sumb_ready, rsum_ready = sem("sumb_ready"), sem("rsum_ready")
        w_ready = sems("w_ready", 2)
        pt_done, pt_copied = sems("pt_done", 3), sems("pt_copied", 3)
        rexp_ready, pv_done, oT_ready = sem("rexp_ready"), sem("pv_done"), sem("oT_ready")
        r_done, xb_ready, x1_ready = sem("r_done"), sem("xb_ready"), sem("x1_ready")
        bn2_ready = sem("bn2_ready")
        var_ready, root_done, rstd_ready = sems("var_ready", 4), sems("root_done", 4), sems("rstd_ready", 4)
        sel_split, scaled_ready, keys_split = sem("sel_split"), sem("scaled_ready"), sem("keys_split")
        magn_ready, magn_shared, exp_ready = sem("magn_ready"), sem("magn_shared"), sem("exp_ready")
        scale_ready, unscale_ready, yscale_ready = sem("scale_ready"), sem("unscale_ready"), sem("yscale_ready")
        x2_ready, xt_done, xhi_ready, xlo_ready = sem("x2_ready"), sem("xt_done"), sem("xhi_ready"), sem("xlo_ready")
        sel_done, egate_ready, gate_steps = sem("sel_done"), sem("egate_ready"), sem("gate_steps")
        gparts_ready, gt_done, gt_ready = sem("gparts_ready"), sem("gt_done"), sem("gt_ready")
        u_done, gb_done, relu_done, hid_ready = sem("u_done"), sem("gb_done"), sem("relu_done"), sem("hid_ready")
        hhi_ready, hlo_ready, down_done = sem("hhi_ready"), sem("hlo_ready"), sem("down_done")
        y_copied, yt_done, y_ready = sem("y_copied"), sem("yt_done"), sem("y_ready")
        stored = sems("stored", 2)

        gate_rest, identb_ready = sem("gate_rest"), sem("identb_ready")
        GATE_STEPS = 12

        def after(eng, semaphore, n):
            if not (isinstance(n, int) and n <= 0):
                eng.wait_ge(semaphore, n)

        def batch(t):
            return 0 <= t < B if isinstance(t, int) else True

        def group(i):
            return 0 <= i < GROUPS if isinstance(i, int) else True

        def steps(eng, step, extra=lambda t: None):
            for t in range(-1, UNROLL):
                step(t, t % 2, lambda d: (t + d) // 2 + 1)
                extra(t)
            with eng.Fori(1, B // UNROLL - 1) as i:
                for j in range(UNROLL):
                    step(i * UNROLL + j, j % 2, lambda d: i * (UNROLL // 2) + ((j + d) // 2 + 1))
            for t in range(B - UNROLL, B + 2):
                step(t, t % 2, lambda d: (t + d) // 2 + 1)
                extra(t)

        def bodies(eng, body):
            for i in range(3):
                body(i, i % 2)
            with eng.Fori(1, GROUPS // 2 - 1) as k:
                body(k * 2 + 1, 1)
                body(k * 2 + 2, 0)
            body(GROUPS - 1, 1)

        block = stack.enter_context(nc.Block())

        @block.sync
        def _(sp):
            sp.dma_start(x_all[:, 0:X_CUTS[1], :], x[:, 0:X_CUTS[1], :]).then_inc(x_in[0], 16)
            for dst, src in ((ident, ident_c), (wq_sb, wq), (wk_sb, wk), (wv_sb, wv), (wo_sb, wo),
                             (remmask, remmask_c), (headmask, headmask_c)):
                sp.dma_start(dst[:], src).then_inc(weights_in, 16)
            column = lambda v: v.rearrange("(d a) -> d a", a=1)
            everywhere = lambda v, m: v.rearrange("(a d) -> a d", a=1).broadcast_to([P, m])
            sp.dma_start(bias_q[:], column(bq)).then_inc(small_in, 16)
            sp.dma_start(bias_k[:], column(bk)).then_inc(small_in, 16)
            sp.dma_start(bv_rows[:], everywhere(bv, D)).then_inc(small_in, 16)
            sp.dma_start(bo_rows[:], everywhere(bo, D)).then_inc(small_in, 16)
            sp.dma_start(gates_in[:, 0:1], everywhere(g_xattn, 1)).then_inc(small_in, 16)
            sp.dma_start(gates_in[:, 1:2], everywhere(g_ffn, 1)).then_inc(small_in, 16)
            def load(t, p):
                row = bass.ds(t, 1)
                if isinstance(t, int) and t == 0:
                    sp.wait_ge(zeroed, 1)
                after(sp, ct_done, t - 1)
                src = ctx_in[row, 0:KMAIN, :].rearrange("o k d -> (o k) d")
                sp.dma_start(ctx_main[0:KMAIN, p, :], src).then_inc(ctx_ld[p], 16)
                sp.dma_start(ctx_main[KMAIN:P, p, :], src).then_inc(ctx_ld[p], 16)
                src = ctx_in[row, KMAIN:KEYS, :].broadcast_to([HALF, KREM, D])
                sp.dma_start(ctx_rem[0:HALF * KREM, p, :], src).then_inc(ctx_ld[p], 16)
                after(sp, negm_ready, t - 1)
                sp.dma_start(mask_in[:, p, :], mask[row].rearrange("o s k -> (o s) k")).then_inc(mask_ld[p], 16)
                after(sp, w_ready[1], t - 1)
                sp.dma_start(prob_g[:, p, :], fside[row].rearrange("o s k -> (o s) k")).then_inc(g_ld[p], 16)

            load(0, 0)
            load(1, 1)
            for c in range(1, len(X_CUTS) - 1):
                cut = slice(X_CUTS[c], X_CUTS[c + 1])
                sp.dma_start(x_all[:, cut, :], x[:, cut, :]).then_inc(x_in[c], 16)
            for dst, src in ((keys_raw, keys), (values_raw, values), (selT, expert_sel), (restart, restart_c),
                             (gatesel_f, gatesel_c)):
                sp.dma_start(dst[:], src).then_inc(experts_in, 16)
            load(2, 0)
            load(3, 1)
            with sp.Fori(1, B // UNROLL) as i:
                for j in range(UNROLL):
                    load(i * UNROLL + j, j % 2)

            outr = out.rearrange("(g j) s d -> s g j d", j=TILES)

            with sp.Fori(0, GROUPS // 2) as k:
                for p in range(2):
                    sp.wait_ge(y_ready, k * 2 + (p + 1))
                    sp.dma_start(outr[:, bass.ds(k * 2 + p, 1)].rearrange("s g j d -> s (g j) d"),
                                 y_out[:, p]).then_inc(stored[p], 16)
            for p in range(2):
                sp.wait_ge(stored[p], 16 * (GROUPS // 2))

        @block.tensor
        def _(pe):
            pe.wait_ge(weights_in, 16 * 7)

            def step(t, p, used):
                q = 1 - p
                if batch(t):
                    pe.wait_ge(q_ready, t + 1)
                    pe.wait_ge(kblk_ready, t + 1)

                def logits(r):
                    if r >= 2:
                        pe.wait_ge(lg_masked[r - 2], t + 1)
                    else:
                        after(pe, lg_masked[r + 2], t)
                    rows = slice(32 * r, 32 * r + 32)
                    pe.matmul(ps[:, bank_lg[r % 2], 0:4 * KEYS], qT[rows, p, :],
                              kblk[rows, p].rearrange("p a b -> p (a b)"),
                              start=True, stop=True).then_inc(lg_done[r], 1)

                def turn(n, u):
                    pe.wait_ge(w_ready[0], u + 1)
                    if n > 0:
                        pe.wait_ge(w_ready[1], u + 1)
                    after(pe, pt_copied[n], u)
                    for c, (kind, m) in enumerate(SETS[n]):
                        src = wrem[:, q, m, :] if kind == "rem" else \
                            wmain[:, q, 2 * m:2 * m + 2, :].rearrange("p a b -> p (a b)")
                        last = pe.transpose(ps[:, bank_pt[n], c * P:(c + 1) * P], src, ident[:])
                    last.then_inc(pt_done[n], 1)

                if batch(t):
                    logits(0)
                    logits(1)
                if batch(t - 1):
                    turn(0, t - 1)
                if batch(t - 2):
                    pe.wait_ge(oT_ready, t - 1)
                    pe.wait_ge(gated_w, 3)
                    pe.matmul(ps[:, bank_o, 2 * P:3 * P], oT[:], wo_g[:], start=True, stop=True).then_inc(r_done, 1)
                if batch(t):
                    logits(2)
                    logits(3)
                if batch(t + 1) or batch(t - 1):
                    o = ps[:, bank_ct, :]
                    after(pe, ct_copied, t + 1)
                    if batch(t + 1):
                        pe.wait_ge(xn_ready, t + 2)
                        pe.wait_ge(ctx_ld[q], used(1) * 48)
                        pe.transpose(o[:, 0:P], xn[:, q, :], ident[:])
                        pe.transpose(o[:, P:2 * P], ctx_main[:, q, :], ident[:])
                        last = pe.transpose(o[:, 2 * P:3 * P], ctx_rem[:, q, :], ident[:])
                    if batch(t - 1):
                        pe.wait_ge(rexp_ready, t)
                        last = pe.transpose(o[:, 3 * P:4 * P], rexp[:].rearrange("p h d -> p (h d)"), ident[:])
                    last.then_inc(ct_done, 1)
                if batch(t - 1):
                    turn(1, t - 1)
                    turn(2, t - 1)
                if batch(t + 1):
                    pe.wait_ge(ct_copied, t + 2)
                    after(pe, v_copied, t + 1)
                    xT, kT = ct[:, q, 0:P], ct[:, q, P + KMAIN:P + KMAIN + KEYS]
                    o = ps[:, bank_proj, :]
                    pe.matmul(o[:, 0:P], wq_sb[:], xT, start=True, stop=True)
                    pe.matmul(o[:, P:P + KEYS], wk_sb[:], kT, start=True, stop=True)
                    pe.matmul(o[:, P + KEYS:2 * P + KEYS], ct[:, q, P:2 * P], wv_sb[:], start=True, stop=True)
                    pe.matmul(o[:, 2 * P + KEYS:3 * P + KEYS], ct[:, q, 2 * P:3 * P], wv_sb[:],
                              start=True, stop=True).then_inc(proj_done, 1)
                if batch(t - 1):
                    pe.wait_ge(vmain_ready, t)
                    pe.wait_ge(vrem_ready, t)
                    after(pe, x1_ready, t - 1)
                    for n in range(3):
                        pe.wait_ge(pt_copied[n], t)
                        for c, (kind, m) in enumerate(SETS[n]):
                            lhsT = vrem[:, q, m * P:(m + 1) * P] if kind == "rem" else vmain[:, q, m * P:(m + 1) * P]
                            last = pe.matmul(ps[:, bank_o, 0:P], lhsT, wT[:, q, 4 * n + c, :],
                                             start=(n == 0 and c == 0), stop=(4 * n + c == len(CHUNKS) - 1))
                    last.then_inc(pv_done, 1)

            def turn_x(i):
                pe.wait_ge(x2_ready, i + 1)
                if isinstance(i, int) and i == 0:
                    pe.wait_ge(v_copied, B)
                after(pe, y_ready, i - 2)
                for j in range(TILES):
                    last = pe.transpose(ps[:, bank_xy, j * P:(j + 1) * P], x2[:, j, :], ident[:])
                last.then_inc(xt_done, 1)

            def select(i, p):
                pe.wait_ge(xhi_ready, i + 1)
                pe.wait_ge(xlo_ready, i + 1)
                if isinstance(i, int) and i == 0:
                    pe.wait_ge(sel_split, 2)
                    pe.wait_ge(ct_copied, B + 2)
                after(pe, gt_ready, i)
                for j in range(TILES):
                    o = ps[:, bank_sg, j * EXPERTS:(j + 1) * EXPERTS]
                    hi, lo = x2_hi[:, p, j * P:(j + 1) * P], x2_lo[:, p, j * P:(j + 1) * P]
                    pe.matmul(o, hi, sel_hi[:], start=True, stop=False)
                    pe.matmul(o, hi, sel_lo[:], start=False, stop=False)
                    last = pe.matmul(o, lo, sel_hi[:], start=False, stop=True)
                last.then_inc(sel_done, 1)

            def turn_g(i):
                pe.wait_ge(gparts_ready, i + 1)
                pe.wait_ge(egate_ready, i + 1)
                o = ps[0:96, bank_sg, 0:GT // 2].bitcast(BF16)
                for j in range(TILES):
                    last = pe.transpose(o[:, j * P:(j + 1) * P], gparts[:, j].rearrange("p a e -> p (a e)"),
                                        identb[:])
                last.then_inc(gt_done, 1)

            def up(i, f, p):
                n = i * BLOCKS + f
                if isinstance(i, int) and i == 0 and f == 0:
                    for r in range(2):
                        pe.wait_ge(lg_masked[2 + r], B)
                        pe.wait_ge(pt_copied[r], B)
                    pe.wait_ge(keys_split, BLOCKS)
                    pe.wait_ge(identb_ready, 2)
                after(pe, relu_done, n - 1)
                w = slice(f * P, (f + 1) * P)
                o = ps[:, bank_u[f % 2], :]
                pe.matmul(o, keys_hi[:, w], x2_hi[:, p, :], start=True, stop=False)
                pe.matmul(o, keys_hi[:, w], x2_lo[:, p, :], start=False, stop=False)
                pe.matmul(o, keys_lo[:, w], x2_hi[:, p, :], start=False, stop=True).then_inc(u_done, 1)
                after(pe, hid_ready, n - 1)
                pe.matmul(ps[:, bank_g[f % 2], :], gatesel[:, 2 * f:2 * f + 2, :].rearrange("p e f -> p (e f)"),
                          gT[:, p, :], start=True, stop=True).then_inc(gb_done, 1)

            def down(i, f, p):
                n = i * BLOCKS + f
                pe.wait_ge(hhi_ready, n + 1)
                pe.wait_ge(hlo_ready, n + 1)
                w, s = slice(f * P, (f + 1) * P), f % LAG
                if f == 0:
                    after(pe, y_copied, i - 1)
                    if isinstance(i, int) and i == 0:
                        pe.wait_ge(pt_copied[2], B)
                    if isinstance(i, int) and i == 1:
                        pe.wait_ge(x1_ready, B)
                o = ps[:, bank_y[p], :]
                pe.matmul(o, values_hi[:, w], hid_hi[:, s, :], start=(f == 0), stop=False)
                pe.matmul(o, values_lo[:, w], hid_hi[:, s, :], start=False, stop=False)
                pe.matmul(o, values_hi[:, w], hid_lo[:, s, :], start=False, stop=(f == BLOCKS - 1)).then_inc(down_done, 1)

            def turn_y(i):
                pe.wait_ge(y_copied, i + 1)
                pe.wait_ge(xlo_ready, min(i + 3, GROUPS) if isinstance(i, int) else i + 3)
                after(pe, y_ready, i)
                for j in range(TILES):
                    last = pe.transpose(ps[:, bank_xy, j * P:(j + 1) * P], yT[:, j * P:(j + 1) * P], ident[:])
                last.then_inc(yt_done, 1)

            def body(i, p):
                pe.wait_ge(gt_ready, i + 1)
                for f in range(BLOCKS):
                    up(i, f, p)
                    if f >= LAG:
                        down(i, f - LAG, p)
                    elif group(i - 1):
                        down(i - 1, BLOCKS + f - LAG, 1 - p)
                    if f == 8 and group(i - 1):
                        turn_y(i - 1)
                    if group(i + 1):
                        if f == 2:
                            turn_x(i + 1)
                        if f == 6:
                            select(i + 1, 1 - p)
                        if f == 14:
                            turn_g(i + 1)

            def extra(t):
                if t == B:
                    turn_x(0)
                    select(0, 0)
                if t == B + 1:
                    turn_g(0)

            steps(pe, step, extra)
            bodies(pe, body)
            for f in range(BLOCKS - LAG, BLOCKS):
                down(GROUPS - 1, f, 1)
            turn_y(GROUPS - 1)

        @block.scalar
        def _(act):
            def root(n, first, last):
                act.wait_ge(var_ready[n], 7)
                act.activation(norm_tmp[:, 5, first:last], norm_tmp[:, 4, first:last], ACT.Sqrt).then_inc(root_done[n], 1)

            act.wait_ge(small_in, 16 * 6)
            act.activation(gates_tanh[:], gates_in[:], ACT.Tanh).then_inc(tanh_done, 1)
            act.activation(bias_qs[:], bias_q[:], ACT.Copy, scale=DH ** -0.5).then_inc(tanh_done, 1)
            root(0, X_CUTS[0], X_CUTS[1])
            act.wait_ge(tanh_done, 2)

            def step(t, p, used):
                q = 1 - p

                def copy_set(n, u):
                    act.wait_ge(pt_done[n], u + 1)
                    after(act, pv_done, u - 1)
                    w = len(SETS[n]) * P
                    act.copy(wT[:, q, 4 * n:4 * n + len(SETS[n]), :].rearrange("p c k -> p (c k)"),
                             ps[:, bank_pt[n], 0:w]).then_inc(pt_copied[n], 1)

                def exponentials(first, last):
                    for h in range(first, last):
                        v = act.activation(soft[:, p, h, :], soft[:, p, h, :], ACT.Exp,
                                           bias=negmax[:, p, h:h + 1], accum_out=sums[:, p, h:h + 1])
                    if last == HALF:
                        v.then_inc(exp_done[0], 1)

                if batch(t - 1):
                    copy_set(0, t - 1)
                    act.wait_ge(rsum_ready, t)
                    after(act, ct_done, t + 1)
                    act.copy(rexp[:], rsum[:, q, :, None].broadcast_to([P, H, DH])).then_inc(rexp_ready, 1)
                if batch(t + 1) or batch(t - 1):
                    act.wait_ge(ct_done, t + 2)
                    after(act, proj_done, t)
                    after(act, oT_ready, t - 2)
                    cols = slice(0 if batch(t + 1) else 3 * P, 4 * P if batch(t - 1) else 3 * P)
                    act.copy(ct[:, q, cols], ps[:, bank_ct, cols]).then_inc(ct_copied, 1)
                if batch(t):
                    act.wait_ge(max_ready[0], t + 1)
                    after(act, rsum_ready, t - 1)
                    exponentials(0, HALF // 2)
                if batch(t - 1):
                    copy_set(1, t - 1)
                    copy_set(2, t - 1)
                if batch(t):
                    exponentials(HALF // 2, HALF)
                if batch(t + 1):
                    act.wait_ge(proj_done, t + 2)
                    after(act, lg_done[3], t)
                    act.activation(qT[:, q, :], ps[:, bank_proj, 0:P], ACT.Identity, scale=DH ** -0.5,
                                   bias=bias_qs[:, 0:1]).then_inc(q_ready, 1)
                    after(act, kblk_ready, t)
                    act.activation(kv[:, q, 0:KEYS], ps[:, bank_proj, P:P + KEYS], ACT.Identity,
                                   bias=bias_k[:, 0:1]).then_inc(k_copied, 1)
                    after(act, vmain_ready, t)
                    after(act, vremm_ready, t)
                    act.copy(kv[:, q, KEYS:], ps[:, bank_proj, P + KEYS:P + KEYS + 2 * P]).then_inc(v_copied, 1)
                if batch(t):
                    act.wait_ge(shifted, t + 1)
                    o = soft[:, p, HALF:H, :].rearrange("p h k -> p (h k)")
                    act.activation(o, o, ACT.Exp).then_inc(exp_done[1], 1)

            def copy_x(i, p):
                act.wait_ge(xt_done, i + 1)
                after(act, u_done, (i - 1) * BLOCKS + 1)
                act.copy(x2_hi[:, p, :], ps[:, bank_xy, :]).then_inc(xhi_ready, 1)

            def gate_exp(i):
                act.wait_ge(sel_done, i + 1)
                after(act, gate_steps, (i - 1) * GATE_STEPS + 1)
                act.activation(egate[:].rearrange("p j e -> p (j e)"), ps[:, bank_sg, 0:TILES * EXPERTS],
                               ACT.Exp, scale=neg_unscale_sel[:, 0:1]).then_inc(egate_ready, 1)

            def copy_g(i, p):
                act.wait_ge(gt_done, i + 1)
                after(act, gb_done, (i - 1) * BLOCKS + 1)
                act.copy(gT[:, p, :], ps[0:96, bank_sg, 0:GT // 2].bitcast(BF16)).then_inc(gt_ready, 1)

            def relu(i, f):
                n = i * BLOCKS + f
                act.wait_ge(u_done, n + 1)
                after(act, hid_ready, n - 1)
                act.activation(relu_u[:, f % 2, :], ps[:, bank_u[f % 2], :], ACT.Relu).then_inc(relu_done, 1)

            def high(i, f):
                n = i * BLOCKS + f
                act.wait_ge(hid_ready, n + 1)
                after(act, down_done, n - LAG + 1)
                act.copy(hid_hi[:, f % LAG, :], hid[:, f % LAG, :]).then_inc(hhi_ready, 1)

            def copy_y(i, p):
                act.wait_ge(down_done, (i + 1) * BLOCKS)
                after(act, yt_done, i)
                act.activation(yT[:], ps[:, bank_y[p], :], ACT.Copy, scale=y_scale[:, 1:2]).then_inc(y_copied, 1)

            def body(i, p):
                for f in range(BLOCKS):
                    relu(i, f)
                    if f > 0:
                        high(i, f - 1)
                    elif group(i - 1):
                        high(i - 1, BLOCKS - 1)
                    if f == 5 and group(i - 1):
                        copy_y(i - 1, 1 - p)
                    if isinstance(i, int) and i == 0 and f == 1:
                        root(3, B // 2, B)
                    if group(i + 1):
                        if f == 3:
                            copy_x(i + 1, 1 - p)
                        if f == 7:
                            gate_exp(i + 1)
                        if f == 14:
                            copy_g(i + 1, 1 - p)

            def extra(t):
                if t == UNROLL - 2:
                    root(1, X_CUTS[1], B)
                if t == B - 1:
                    root(2, 0, B // 2)
                if t == B:
                    copy_x(0, 0)
                if t == B + 1:
                    act.wait_ge(unscale_ready, 2)
                    gate_exp(0)
                    copy_g(0, 0)
                    act.wait_ge(yscale_ready, 2)

            steps(act, step, extra)
            bodies(act, body)
            high(GROUPS - 1, BLOCKS - 1)
            copy_y(GROUPS - 1, 1)

        @block.vector
        def _(dve):
            dve.memset(ctx_rem[96:P], 0.0).then_inc(zeroed, 1)
            dve.memset(wrem[:], 0.0).then_inc(zeroed, 1)
            dve.memset(vmain[:], 0.0).then_inc(zeroed, 1)
            dve.memset(vrem[:], 0.0).then_inc(zeroed, 1)
            def token_stats(first, last):
                n = 4
                with dve.Fori(0, (last - first) // n) as k:
                    for j in range(n):
                        b = bass.ds(k * n + (first + j), 1)
                        dve.bn_stats(bn1[:, b, :].rearrange("p o d -> p (o d)"),
                                     x_all[:, b, :].rearrange("p o d -> p (o d)")).then_inc(bn1_ready, 1)

            def variance(n, bn, mean, first, last):
                cut, done = slice(first, last), var_ready[n]
                mean_sum, mean_diff, sq_sum, sq_diff, var_eps = (norm_tmp[:, k, cut] for k in range(5))
                me, qe, mo, qo = (bn[:, cut, k] for k in (1, 2, 4, 5))
                dve.tensor_tensor(mean_sum, me, mo, ALU.add).then_inc(done, 1)
                dve.tensor_tensor(mean_diff, me, mo, ALU.subtract).then_inc(done, 1)
                dve.tensor_tensor(sq_sum, qe, qo, ALU.add).then_inc(done, 1)
                dve.wait_ge(done, 1)
                dve.tensor_scalar(mean[:, cut], mean_sum, 0.5, None, ALU.mult).then_inc(done, 1)
                dve.wait_ge(done, 2)
                dve.scalar_tensor_tensor(sq_diff, mean_diff, 0.25, mean_diff, ALU.mult, ALU.mult).then_inc(done, 1)
                dve.wait_ge(done, 5)
                dve.scalar_tensor_tensor(var_eps, sq_sum, 1.0 / D, sq_diff, ALU.mult, ALU.add).then_inc(done, 1)
                dve.wait_ge(done, 6)
                dve.tensor_scalar(var_eps, var_eps, EPS, None, ALU.add).then_inc(done, 1)

            def rstd(n, out, first, last):
                cut, ready = slice(first, last), rstd_ready[n]
                var_eps, root, y, z = (norm_tmp[:, k, cut] for k in range(4, 8))
                dve.wait_ge(root_done[n], 1)
                dve.reciprocal(y, root).then_inc(ready, 1)
                dve.wait_ge(ready, 1)
                dve.tensor_tensor(z, y, y, ALU.mult).then_inc(ready, 1)
                dve.wait_ge(ready, 2)
                dve.tensor_tensor(z, z, var_eps, ALU.mult).then_inc(ready, 1)
                dve.wait_ge(ready, 3)
                dve.tensor_scalar(z, z, -0.5, 1.5, ALU.mult, ALU.add).then_inc(ready, 1)
                dve.wait_ge(ready, 4)
                dve.tensor_tensor(out[:, cut], y, z, ALU.mult).then_inc(ready, 1)
                dve.wait_ge(ready, 5)

            dve.wait_ge(x_in[0], 16)
            token_stats(X_CUTS[0], X_CUTS[1])
            dve.wait_ge(bn1_ready, X_CUTS[1])
            variance(0, bn1, mean1, X_CUTS[0], X_CUTS[1])
            dve.wait_ge(weights_in, 16 * 7)
            dve.wait_ge(small_in, 16 * 6)
            dve.wait_ge(tanh_done, 1)
            dve.tensor_scalar(wo_g[:], wo_sb[:], gates_tanh[:, 0:1], None, ALU.mult).then_inc(gated_w, 1)
            dve.tensor_scalar(bo_g[:], bo_rows[:], gates_tanh[:, 0:1], None, ALU.mult).then_inc(gated_w, 1)
            dve.tensor_tensor(bv_rem[:], bv_rows[:], remmask[:], ALU.mult).then_inc(gated_w, 1)
            rstd(0, rstd1, X_CUTS[0], X_CUTS[1])
            dve.wait_ge(zeroed, 4)

            def step(t, p, used):
                q = 1 - p

                def masked(r):
                    dve.wait_ge(lg_done[r], t + 1)
                    dve.tensor_tensor(soft[:, p, 4 * r:4 * r + 4, :],
                                      ps[:, bank_lg[r % 2], 0:4 * KEYS].rearrange("p (h k) -> p h k", h=4),
                                      negm[:, p, None, :].broadcast_to([P, 4, KEYS]), ALU.add).then_inc(lg_masked[r], 1)

                def negated_max(m):
                    dve.wait_ge(lg_masked[2 * m + 1], t + 1)
                    dve.tensor_reduce(negmax[:, p, HALF * m:HALF * m + HALF], soft[:, p, HALF * m:HALF * m + HALF, :],
                                      AX.X, ALU.max, negate=True).then_inc(max_ready[m], 1)

                if batch(t - 2):
                    dve.wait_ge(pv_done, t - 1)
                    dve.wait_ge(ct_copied, t + 1)
                    after(dve, r_done, t - 2)
                    dve.tensor_tensor(oT[:], ps[:, bank_o, 0:P], ct[:, p, 3 * P:4 * P], ALU.mult).then_inc(oT_ready, 1)
                if batch(t):
                    dve.wait_ge(negm_ready, t + 1)
                    after(dve, w_ready[1], t - 1)
                    masked(0)
                if batch(t - 1):
                    dve.wait_ge(exp_done[1], t)
                    dve.tensor_reduce(sums[:, q, HALF:H], soft[:, q, HALF:H, :], AX.X, ALU.add).then_inc(sumb_ready, 1)
                if batch(t):
                    masked(1)
                if batch(t + 1):
                    after(dve, ct_done, t)
                    b = bass.ds(t + 1, 1)
                    dve.tensor_scalar(xn[:, q, :], x_all[:, b, :].rearrange("p o d -> p (o d)"), mean1[:, b], rstd1[:, b],
                                      ALU.subtract, ALU.mult).then_inc(xn_ready, 1)
                if batch(t - 1):
                    dve.wait_ge(sumb_ready, t)
                    dve.wait_ge(exp_done[0], t)
                    after(dve, rexp_ready, t - 2)
                    dve.reciprocal(rsum[:, q, :], sums[:, q, :]).then_inc(rsum_ready, 1)
                if batch(t):
                    after(dve, exp_done[0], t - 1)
                    negated_max(0)
                if batch(t - 2):
                    b = bass.ds(t - 2, 1)
                    dve.wait_ge(r_done, t - 1)
                    dve.wait_ge(xb_ready, t - 1)
                    dve.tensor_tensor(x_all[:, b, :].rearrange("p o d -> p (o d)"), ps[:, bank_o, 2 * P:3 * P], xb[:, p, :],
                                      ALU.add).then_inc(x1_ready, 1)
                if batch(t):
                    masked(2)
                    masked(3)
                if batch(t - 2):
                    dve.wait_ge(x1_ready, t - 1)
                if batch(t):
                    negated_max(1)
                if batch(t - 2):
                    dve.bn_stats(bn2[:, b, :].rearrange("p o d -> p (o d)"),
                                 x_all[:, b, :].rearrange("p o d -> p (o d)")).then_inc(bn2_ready, 1)
                if batch(t):
                    dve.wait_ge(max_ready[1], t + 1)
                    dve.tensor_tensor(soft[:, p, HALF:H, :], soft[:, p, HALF:H, :],
                                      negmax[:, p, HALF:H, None].broadcast_to([P, HALF, KEYS]), ALU.add).then_inc(shifted, 1)
                if batch(t):
                    after(dve, pv_done, t - 1)
                    dve.wait_ge(v_copied, t + 1)
                    for e in range(2):
                        rows = slice(KMAIN * e, KMAIN * e + KMAIN)
                        pairs = lambda v: v.rearrange("p (m e d) -> p m e d", e=2, d=DH)[:, :, e, :]
                        v = dve.tensor_tensor(vmain[rows, p, :].rearrange("p (m w) -> p m w", w=MAIN_STEP)[:, :, DH * e:DH * e + DH],
                                              pairs(kv[rows, p, KEYS:KEYS + P]), pairs(bv_rows[rows]), ALU.add)
                    v.then_inc(vmain_ready, 1)
                    after(dve, vrem_ready, t - 1)
                    dve.tensor_tensor(vrem_m[:, p, :], kv[:, p, KEYS + P:KEYS + 2 * P], remmask[:], ALU.mult).then_inc(vremm_ready, 1)
                if batch(t + 1):
                    dve.wait_ge(k_copied, t + 2)
                    after(dve, lg_done[3], t)
                    dve.tensor_tensor(kblk[:, q], kv[:, q, None, 0:KEYS].broadcast_to([P, 4, KEYS]),
                                      headmask[:, :, None].broadcast_to([P, 4, KEYS]), ALU.mult).then_inc(kblk_ready, 1)

            def scales():
                dve.wait_ge(experts_in, 16 * 5)
                for n, src in enumerate((keys_raw, values_raw, selT)):
                    dve.tensor_reduce(magn[:, n:n + 1], src[:], AX.X, ALU.max,
                                      apply_absolute_value=True).then_inc(magn_ready, 1)

            def more_scales():
                dve.wait_ge(magn_shared, 1)
                dve.tensor_scalar(magn_exp[:], magn_all[:].bitcast(I32), EXP_MASK, None, ALU.bitwise_and).then_inc(exp_ready, 1)
                dve.wait_ge(exp_ready, 1)
                dve.tensor_scalar(magn_exp[:], magn_exp[:], float(LEAST_EXP << 23), None, ALU.max).then_inc(exp_ready, 1)
                dve.wait_ge(exp_ready, 2)
                dve.tensor_scalar(scale_w[:].bitcast(I32), magn_exp[:], -1.0, float((254 + SCALED_EXP) << 23),
                                  ALU.mult, ALU.add).then_inc(scale_ready, 1)
                dve.tensor_scalar(unscale_w[:].bitcast(I32), magn_exp[:], float(-(SCALED_EXP << 23)), None,
                                  ALU.add).then_inc(unscale_ready, 1)
                dve.wait_ge(scale_ready, 1)
                dve.tensor_scalar(sel_hi[:], selT[:], scale_w[:, 2:3], None, ALU.mult).then_inc(sel_split, 1)
                dve.wait_ge(sel_split, 1)
                dve.scalar_tensor_tensor(sel_lo[:], selT[:], scale_w[:, 2:3], sel_hi[:], ALU.mult, ALU.subtract).then_inc(sel_split, 1)
                dve.wait_ge(unscale_ready, 1)
                dve.tensor_scalar(neg_unscale_sel[:], unscale_w[:, 2:3], -1.0, None, ALU.mult).then_inc(unscale_ready, 1)
                dve.tensor_scalar(y_scale[:, 0:1], unscale_w[:, 0:1], unscale_w[:, 1:2], 1 / HIDDEN_SHIFT,
                                  ALU.mult, ALU.mult).then_inc(yscale_ready, 1)
                dve.wait_ge(yscale_ready, 1)
                dve.tensor_scalar(y_scale[:, 1:2], y_scale[:, 0:1], gates_tanh[:, 1:2], None, ALU.mult).then_inc(yscale_ready, 1)

            def normed(i):
                after(dve, xt_done, i)
                for j in range(TILES):
                    b = bass.ds(i * TILES + j, 1)
                    v = dve.tensor_scalar(x2[:, j, :], x_all[:, b, :].rearrange("p o d -> p (o d)"), mean2[:, b],
                                          rstd2[:, b], ALU.subtract, ALU.mult)
                v.then_inc(x2_ready, 1)

            def low_x(i, p):
                dve.wait_ge(xhi_ready, i + 1)
                after(dve, u_done, (i - 1) * BLOCKS + 1)
                dve.tensor_tensor(x2_lo[:, p, :], ps[:, bank_xy, :], x2_hi[:, p, :], ALU.subtract).then_inc(xlo_ready, 1)

            def chain(i, k):
                dve.wait_ge(gate_steps, i * GATE_STEPS + k)

            def gates(i):
                dve.wait_ge(egate_ready, i + 1)
                dve.tensor_scalar(dgate[:], egate[:], 1.0, None, ALU.add).then_inc(gate_steps, 1)
                chain(i, 1)
                dve.reciprocal(gate[:], dgate[:]).then_inc(gate_steps, 1)
                chain(i, 2)

            def gates_top(i):
                fourth = best[:, :, TOP - 1:TOP].broadcast_to([P, TILES, EXPERTS])
                for j in range(TILES):
                    v = dve.max(best[:, j, :], gate[:, j, :])
                v.then_inc(gate_steps, 1)
                chain(i, 3)
                dve.tensor_tensor(above[:], gate[:], fourth, ALU.is_gt).then_inc(gate_steps, 1)
                dve.tensor_tensor(equal[:], gate[:], fourth, ALU.is_equal).then_inc(gate_steps, 1)

            def gates_more(i):
                chain(i, 4)
                dve.tensor_reduce(n_above[:], above[:], AX.X, ALU.add).then_inc(gate_steps, 1)
                chain(i, 5)
                dve.tensor_tensor_scan(rank[:].rearrange("p j e -> p (j e)"), restart[:],
                                       equal[:].rearrange("p j e -> p (j e)"), 0.0, ALU.mult, ALU.add).then_inc(gate_steps, 1)
                chain(i, 7)
                dve.tensor_tensor(rank2[:], rank[:], n_above[:, :, None].broadcast_to([P, TILES, EXPERTS]),
                                  ALU.add).then_inc(gate_steps, 1)
                chain(i, 8)
                dve.scalar_tensor_tensor(taken[:], rank2[:], float(TOP), equal[:], ALU.is_le, ALU.mult).then_inc(gate_steps, 1)
                chain(i, 9)
                dve.tensor_tensor(kept[:], taken[:], above[:], ALU.add).then_inc(gate_steps, 1)
                chain(i, 10)
                after(dve, gt_done, i)
                dve.tensor_tensor(gsel[:], kept[:], gate[:], ALU.mult).then_inc(gate_steps, 1)

            def split_gates(i):
                chain(i, 11)
                dve.tensor_copy(gparts[:, :, 0, :], gsel[:]).then_inc(gate_steps, 1)
                chain(i, 12)
                dve.tensor_tensor(grest1[:], gsel[:], gparts[:, :, 0, :], ALU.subtract).then_inc(gate_rest, 1)
                dve.wait_ge(gate_rest, i * 3 + 1)
                dve.tensor_copy(gparts[:, :, 1, :], grest1[:]).then_inc(gate_rest, 1)
                dve.wait_ge(gate_rest, i * 3 + 2)
                dve.tensor_tensor(grest2[:], grest1[:], gparts[:, :, 1, :], ALU.subtract).then_inc(gate_rest, 1)
                dve.wait_ge(gate_rest, i * 3 + 3)
                dve.tensor_copy(gparts[:, :, 2, :], grest2[:]).then_inc(gparts_ready, 1)

            def hidden(i, f):
                n = i * BLOCKS + f
                dve.wait_ge(relu_done, n + 1)
                dve.wait_ge(gb_done, n + 1)
                after(dve, hlo_ready, n - LAG + 1)
                dve.tensor_tensor(hid[:, f % LAG, :], relu_u[:, f % 2, :], ps[:, bank_g[f % 2], :],
                                  ALU.mult).then_inc(hid_ready, 1)

            def residual(i, p, uses):
                dve.wait_ge(yt_done, i + 1)
                after(dve, stored[p], uses * 16)
                dve.tensor_tensor(y_out[:, p], ps[:, bank_xy, :].rearrange("p (j d) -> p j d", j=TILES),
                                  x_all[:, bass.ds(i * TILES, TILES), :], ALU.add).then_inc(y_ready, 1)

            def body(i, p, uses):
                for f in range(BLOCKS):
                    hidden(i, f)
                    if f == 10 and group(i - 1):
                        residual(i - 1, 1 - p, uses)
                    if isinstance(i, int) and i == 0 and f == 3:
                        rstd(3, rstd2, B // 2, B)
                    if group(i + 1):
                        if f == 0:
                            normed(i + 1)
                        if f == 3:
                            low_x(i + 1, 1 - p)
                        if f == 7:
                            gates(i + 1)
                        if f == 8:
                            gates_top(i + 1)
                        if f == 9:
                            gates_more(i + 1)
                        if f == 11:
                            split_gates(i + 1)

            def extra(t):
                if t == -1:
                    dve.wait_ge(x_in[1], 16)
                    token_stats(X_CUTS[1], X_CUTS[2])
                if t == 0:
                    dve.wait_ge(x_in[2], 16)
                    token_stats(X_CUTS[2], X_CUTS[3])
                    dve.wait_ge(bn1_ready, B)
                if t == 1:
                    variance(1, bn1, mean1, X_CUTS[1], B)
                    scales()
                if t == 3:
                    rstd(1, rstd1, X_CUTS[1], B)
                    more_scales()
                if t == B - 2:
                    dve.wait_ge(bn2_ready, B // 2)
                    variance(2, bn2, mean2, 0, B // 2)
                if t == B:
                    rstd(2, rstd2, 0, B // 2)
                    normed(0)
                    low_x(0, 0)
                if t == B + 1:
                    gates(0)
                    gates_top(0)
                    gates_more(0)
                    split_gates(0)
                    dve.wait_ge(bn2_ready, B)
                    variance(3, bn2, mean2, B // 2, B)

            steps(dve, step, extra)
            body(0, 0, 0)
            body(1, 1, 0)
            body(2, 0, 0)
            with dve.Fori(1, GROUPS // 2 - 1) as k:
                body(k * 2 + 1, 1, k)
                body(k * 2 + 2, 0, k)
            body(GROUPS - 1, 1, GROUPS // 2 - 1)
            residual(GROUPS - 1, 1, GROUPS // 2 - 1)

        @block.gpsimd
        def _(pool):
            pool.wait_ge(zeroed, 4)
            pool.wait_ge(weights_in, 16 * 7)
            pool.tensor_copy(identb[:], ident[:]).then_inc(identb_ready, 1)
            pool.wait_ge(gated_w, 3)

            def step(t, p, used):
                q = 1 - p

                def weights(m, u, up, uses):
                    hs = slice(HALF * m, HALF * m + HALF)
                    pool.wait_ge(exp_done[m], u + 1)
                    pool.wait_ge(g_ld[up], uses * 16)
                    after(pool, pt_done[2], u - 1)
                    pool.tensor_tensor(wmain[:, up, hs, :], soft[:, up, hs, 0:KMAIN],
                                       prob_g[:, up, None, 0:KMAIN].broadcast_to([P, HALF, KMAIN]), ALU.mult)
                    pool.tensor_tensor(wrem[:, up, m, 0:HALF * KREM].rearrange("p (h k) -> p h k", h=HALF),
                                       soft[:, up, hs, KMAIN:KEYS],
                                       prob_g[:, up, None, KMAIN:KEYS].broadcast_to([P, HALF, KREM]), ALU.mult).then_inc(w_ready[m], 1)

                if batch(t + 1):
                    pool.wait_ge(mask_ld[q], used(1) * 16)
                    after(pool, lg_masked[3], t)
                if batch(t - 1):
                    weights(1, t - 1, q, used(-1))
                if batch(t + 1):
                    pool.tensor_scalar(negm[:, q, :], mask_in[:, q, :], -1.0, 1e9, ALU.add, ALU.mult).then_inc(negm_ready, 1)
                if batch(t - 2):
                    after(pool, x1_ready, t - 3)
                    pool.tensor_tensor(xb[:, p, :], x_all[:, bass.ds(t - 2, 1), :].rearrange("p o d -> p (o d)"), bo_g[:],
                                       ALU.add).then_inc(xb_ready, 1)
                if batch(t):
                    weights(0, t, p, used(0))
                    pool.wait_ge(vremm_ready, t + 1)
                    after(pool, pv_done, t - 1)
                    halves = lambda v: v.rearrange("p (m w) -> p m w", m=2)
                    pool.tensor_tensor(halves(vrem[:, p, :])[:, :, 0:HALF * DH], halves(vrem_m[:, p, :]), halves(bv_rem[:]),
                                       ALU.add).then_inc(vrem_ready, 1)

            def split_weights(i, cut):
                pairs = ((0, keys_raw, keys_hi, keys_lo), (1, values_raw, values_hi, values_lo))
                for n, src, hi, lo in pairs:
                    scale = scale_w[:, n:n + 1].broadcast_to([P, P])
                    pool.tensor_tensor(hi[:, cut], src[:, cut], scale, ALU.mult)
                    pool.tensor_tensor(scaled[:, n, :], src[:, cut], scale, ALU.mult).then_inc(scaled_ready, 1)
                pool.wait_ge(scaled_ready, i * 2 + 2)
                for n, src, hi, lo in pairs:
                    v = pool.tensor_tensor(lo[:, cut], scaled[:, n, :], hi[:, cut], ALU.subtract)
                v.then_inc(keys_split, 1)


            def body(i, p):
                for f in range(BLOCKS):
                    n = i * BLOCKS + f
                    pool.wait_ge(hid_ready, n + 1)
                    pool.wait_ge(hhi_ready, n + 1)
                    after(pool, down_done, n - LAG + 1)
                    pool.tensor_tensor(hid_lo[:, f % LAG, :], hid[:, f % LAG, :], hid_hi[:, f % LAG, :],
                                       ALU.subtract).then_inc(hlo_ready, 1)

            def extra(t):
                if t == 1:
                    pool.wait_ge(experts_in, 16 * 5)
                    pool.tensor_copy(gatesel[:], gatesel_f[:, :, None].broadcast_to([96, EXPERTS, FE])).then_inc(identb_ready, 1)
                if t == 2:
                    pool.wait_ge(magn_ready, 3)
                    pool.partition_all_reduce(magn_all[:], magn[:], P, ABSMAX).then_inc(magn_shared, 1)
                if t == 3:
                    pool.wait_ge(scale_ready, 1)

            for t in range(-1, UNROLL):
                step(t, t % 2, lambda d: (t + d) // 2 + 1)
                extra(t)
            split_weights(0, slice(0, P))
            with pool.Fori(1, B // UNROLL - 1) as i:
                for j in range(UNROLL):
                    step(i * UNROLL + j, j % 2, lambda d: i * (UNROLL // 2) + ((j + d) // 2 + 1))
                    if j == 1:
                        split_weights(i, bass.ds(i * P, P))
            for t in range(B - UNROLL, B + 2):
                step(t, t % 2, lambda d: (t + d) // 2 + 1)
                if t == B - UNROLL:
                    split_weights(BLOCKS - 1, slice((BLOCKS - 1) * P, BLOCKS * P))
            bodies(pool, body)


_INS = ["x", "ctx_1024", "fside_BxSxS2_0", "mask_BxSxS2_ik1", "g_xattn", "g_ffn",
        "L0_xattn_wq_k", "L0_xattn_wq_b", "L0_xattn_wk_k", "L0_xattn_wk_b", "L0_xattn_wv_k", "L0_xattn_wv_b",
        "L0_xattn_wo_k", "L0_xattn_wo_b", "L0_ffn_expert_sel", "L0_ffn_keys", "L0_ffn_values"]


def shape_constants():
    part, col = np.arange(P)[:, None], np.arange(P)[None, :]
    headmask = (part % 32 // DH == np.arange(4)[None, :]).astype(np.float32)
    remmask = (part // KREM == col // DH % HALF).astype(np.float32)
    gatesel = ((np.arange(96)[:, None] % EXPERTS == np.arange(EXPERTS)[None, :]) * HIDDEN_SHIFT).astype(np.float32)
    restart = np.broadcast_to((col % EXPERTS != 0), (P, P)).astype(np.float32)
    return {"c_ident": np.eye(P, dtype=np.float32), "c_headmask": headmask, "c_remmask": remmask,
            "c_gatesel": gatesel, "c_restart": np.ascontiguousarray(restart)}


def kernel(**inputs):
    import concourse.bacc as bacc
    from concourse.bass_utils import run_bass_kernel_spmd

    nc = bacc.Bacc("TRN2", target_bir_lowering=False, num_devices=1)
    given = dict(inputs)
    given["x"] = inputs["x"].transpose(1, 0, 2)
    given["L0_ffn_expert_sel"] = inputs["L0_ffn_expert_sel"].T
    given["L0_ffn_keys"] = inputs["L0_ffn_keys"].transpose(1, 0, 2).reshape(D, EXPERTS * FE)
    given["L0_ffn_values"] = inputs["L0_ffn_values"].reshape(BLOCKS, P, D).transpose(1, 0, 2).reshape(P, BLOCKS * D)
    arrays = {f"in_{n}": np.ascontiguousarray(given[n]) for n in _INS} | shape_constants()
    args = [nc.dram_tensor(n, a.shape, mybir.dt.from_np(a.dtype), kind="ExternalInput").ap() for n, a in arrays.items()]
    out = nc.dram_tensor("out_0", (B, S, D), F32, kind="ExternalOutput").ap()
    build(nc, *args, out)
    result = run_bass_kernel_spmd(nc, [arrays], core_ids=[0])
    return result.results[0]["out_0"]
```

```python
from contextlib import ExitStack

import numpy as np
import concourse.bass as bass
from concourse import mybir

F32 = mybir.dt.float32
F16 = mybir.dt.float16
BF16 = mybir.dt.bfloat16
I32 = mybir.dt.int32
U16 = mybir.dt.uint16
ALU = mybir.AluOpType
ACT = mybir.ActivationFunctionType
AX = mybir.AxisListType
ABSMAX = bass.bass_isa.ReduceOp.absmax

P = 128
B, S, D = 64, 128, 128
KEYS = 77
H, DH = 16, 8
QUADS = 4
KMAIN = 64
KREM = KEYS - KMAIN
HALF = H // 2
EXPERTS, FE, TOP = 32, 64, 4
BLOCKS = EXPERTS * FE // P
TILES = 4
GROUPS = B // TILES
GT = TILES * P
UNROLL = 4
LAG = 4
NEAR = 6
FAR_CUT = 2
X_CUTS = [0, 8, 16, 40, 64]
EARLY = 40
MID = 7
FIRST = 24
MAIN_STEP = P + 2 * DH
CTX_COLS = 2 * P
REM_STEP = P + HALF * DH
EPS = 1e-5
HIDDEN_SHIFT = 2.0 ** -5
SCALED_EXP = 12
LEAST_EXP = 20
EXP_MASK = 0x7F800000

CHUNKS = [("rem", 0), ("main", 0), ("main", 1), ("main", 2),
          ("main", 3), ("rem", 1), ("main", 4), ("main", 5),
          ("main", 6), ("main", 7)]
SETS = [CHUNKS[0:4], CHUNKS[4:8], CHUNKS[8:10]]


def build(nc, x, ctx_in, fside, mask, g_xattn, g_ffn, wq, bq, wk, bk, wv, bv, wo, bo,
          expert_sel, keys, values, ident_c, headmask_c, remmask_c, gatesel_c, restart_c, out, gates_dram):
    with ExitStack() as stack:
        def sb(name, shape, dt=F32):
            return stack.enter_context(nc.sbuf_tensor(name, shape, dt))

        def sem(name):
            return stack.enter_context(nc.semaphore(name))

        def sems(name, n):
            return [sem(f"{name}{i}") for i in range(n)]

        ps = stack.enter_context(nc.psum_tensor("ps", [P, 8, 512], F32))
        bank_ct, bank_proj, bank_lg, bank_pt, bank_o = 0, 1, (2, 3), (4, 5, 6), 7
        bank_sg, bank_xy, bank_u, bank_g, bank_y = 2, 1, (3, 0), (4, 5), (6, 7)

        ident = sb("ident", [P, P])
        zeros = sb("zeros", [P, 2 * P])
        identb = sb("identb", [P, P], BF16)
        headmask = sb("headmask", [P, 4])
        remmask = sb("remmask", [P, P])
        gates_all = sb("gates_all", [EXPERTS, GT])
        gates_far = sb("gates_far", [P, BLOCKS - NEAR, GT])
        gatesel = sb("gatesel", [96, EXPERTS, FE], U16)
        restart = sb("restart", [P, P])
        wq_sb, wk_sb, wv_sb, wo_sb = (sb(n, [P, P]) for n in ("wq_sb", "wk_sb", "wv_sb", "wo_sb"))
        wo_g = sb("wo_g", [P, P])
        bias_q, bias_k, bias_qs = sb("bias_q", [P, 1]), sb("bias_k", [P, 1]), sb("bias_qs", [P, 1])
        bv_rows, bo_rows = sb("bv_rows", [P, P]), sb("bo_rows", [P, P])
        bv_rem, bo_g = sb("bv_rem", [P, P]), sb("bo_g", [P, P])
        gates_in, gates_tanh = sb("gates_in", [P, 2]), sb("gates_tanh", [P, 2])
        keys_raw = sb("keys_raw", [P, EXPERTS * FE])
        values_raw = sb("values_raw", [P, BLOCKS * P])
        keys_hi, keys_lo = sb("keys_hi", [P, EXPERTS * FE], F16), sb("keys_lo", [P, EXPERTS * FE], F16)
        values_hi, values_lo = sb("values_hi", [P, BLOCKS * P], F16), sb("values_lo", [P, BLOCKS * P], F16)
        selT = sb("selT", [P, EXPERTS])
        sel_hi, sel_lo = sb("sel_hi", [P, EXPERTS], F16), sb("sel_lo", [P, EXPERTS], F16)
        magn, magn_all = sb("magn", [P, 3]), sb("magn_all", [P, 3])
        magn_exp = sb("magn_exp", [P, 3], I32)
        scaled = sb("scaled", [P, 2, P])
        scale_w, unscale_w = sb("scale_w", [P, 3]), sb("unscale_w", [P, 3])
        neg_unscale_sel, y_scale = sb("neg_unscale_sel", [P, 1]), sb("y_scale", [P, 2])

        x_all = sb("x_all", [P, B, D])
        bn1, bn2 = sb("bn1", [P, B, 6]), sb("bn2", [P, B, 6])
        mean1, mean2 = sb("mean1", [P, B]), sb("mean2", [P, B])
        rstd1, rstd2 = sb("rstd1", [P, B]), sb("rstd2", [P, B])
        norm_tmp = sb("norm_tmp", [P, 8, B])

        ctxT = sb("ctxT", [P, 2, CTX_COLS])
        prob_g = sb("prob_g", [P, 2, KEYS])
        mask_in = sb("mask_in", [P, 2, KEYS], I32)
        negm = sb("negm", [P, 2, KEYS])
        xn = sb("xn", [P, 2, D])
        ct = sb("ct", [P, 2, 2 * P])
        qT = sb("qT", [P, 2, P])
        kv = sb("kv", [P, 2, KEYS + 2 * P])
        kblk = sb("kblk", [P, 2, 4, KEYS])
        vmain = sb("vmain", [P, 2, HALF * MAIN_STEP])
        vrem_m, vrem = sb("vrem_m", [P, 2, P]), sb("vrem", [P, 2, 2 * REM_STEP])
        soft = sb("soft", [P, 2, H, KEYS])
        negmax, sums = sb("negmax", [P, 2, H]), sb("sums", [P, 2, H])
        rsum = sb("rsum", [P, 2, H])
        wmain, wrem = sb("wmain", [P, 2, H, KMAIN]), sb("wrem", [P, 2, 2, P])
        wT = sb("wT", [P, 2, len(CHUNKS), P])
        rexp = sb("rexp", [P, H, DH])
        oT = sb("oT", [P, P])
        xb = sb("xb", [P, 2, D])

        x2 = sb("x2", [P, TILES, D])
        x2_hi, x2_lo = sb("x2_hi", [P, 2, GT], F16), sb("x2_lo", [P, 2, GT], F16)
        egate, gate = sb("egate", [P, TILES, EXPERTS]), sb("gate", [P, TILES, EXPERTS])
        dgate = sb("dgate", [P, TILES, EXPERTS])
        best = sb("best", [P, TILES, 8])
        above, equal = sb("above", [P, TILES, EXPERTS]), sb("equal", [P, TILES, EXPERTS])
        n_above, rank = sb("n_above", [P, TILES]), sb("rank", [P, TILES, EXPERTS])
        rank2, taken = sb("rank2", [P, TILES, EXPERTS]), sb("taken", [P, TILES, EXPERTS])
        kept, gsel = sb("kept", [P, TILES, EXPERTS]), sb("gsel", [P, TILES, EXPERTS])
        grest1, grest2 = sb("grest1", [P, TILES, EXPERTS]), sb("grest2", [P, TILES, EXPERTS])
        gparts = sb("gparts", [P, TILES, 3, EXPERTS], BF16)
        gT = sb("gT", [96, 2, GT], BF16)
        relu_u = sb("relu_u", [P, 2, GT])
        hid = sb("hid", [P, LAG, GT])
        hid_hi, hid_lo = sb("hid_hi", [P, LAG, GT], F16), sb("hid_lo", [P, LAG, GT], F16)
        yT, y_out = sb("yT", [P, GT]), sb("y_out", [P, 2, TILES, D])

        weights_in, small_in = sem("weights_in"), sem("small_in")
        x_in = sems("x_in", len(X_CUTS) - 1)
        keys_in, values_in, late_in = sem("keys_in"), sem("values_in"), sem("late_in")
        zeros_ready = sem("zeros_ready")
        zeroed, vzeroed, tanh_done, gated_w = sem("zeroed"), sem("vzeroed"), sem("tanh_done"), sem("gated_w")
        bn1_ready = sem("bn1_ready")
        ctx_ld, g_ld, mask_ld = sems("ctx_ld", 2), sems("g_ld", 2), sems("mask_ld", 2)
        negm_ready, xn_ready = sem("negm_ready"), sem("xn_ready")
        ct_done, ct_copied, proj_done = sem("ct_done"), sem("ct_copied"), sem("proj_done")
        q_ready, k_copied, v_copied = sem("q_ready"), sem("k_copied"), sem("v_copied")
        kblk_ready, vmain_ready = sem("kblk_ready"), sem("vmain_ready")
        vremm_ready, vrem_ready = sem("vremm_ready"), sem("vrem_ready")
        lg_done, lg_masked = sems("lg_done", QUADS), sems("lg_masked", QUADS)
        max_ready = sems("max_ready", 2)
        shifted, exp_done = sem("shifted"), sems("exp_done", 2)
        sumb_ready, rsum_ready = sem("sumb_ready"), sem("rsum_ready")
        w_ready = sems("w_ready", 2)
        pt_done, pt_copied = sems("pt_done", 3), sems("pt_copied", 3)
        rexp_ready, pv_done, oT_ready = sem("rexp_ready"), sem("pv_done"), sem("oT_ready")
        r_done, xb_ready, x1_ready = sem("r_done"), sem("xb_ready"), sem("x1_ready")
        bn2_ready = sem("bn2_ready")
        var_ready, root_done, rstd_ready = sems("var_ready", 5), sems("root_done", 5), sems("rstd_ready", 5)
        sel_split, scaled_ready, keys_split = sem("sel_split"), sem("scaled_ready"), sem("keys_split")
        magn_ready, magn_shared, exp_ready = sem("magn_ready"), sem("magn_shared"), sem("exp_ready")
        scale_ready, unscale_ready, yscale_ready = sem("scale_ready"), sem("unscale_ready"), sem("yscale_ready")
        x2_ready, xt_done, xhi_ready, xlo_ready = sem("x2_ready"), sem("xt_done"), sem("xhi_ready"), sem("xlo_ready")
        sel_done, egate_ready, gate_steps = sem("sel_done"), sem("egate_ready"), sem("gate_steps")
        gparts_ready, gt_done, gt_ready = sem("gparts_ready"), sem("gt_done"), sem("gt_ready")
        u_done, gb_done, relu_done, hid_ready = sem("u_done"), sem("gb_done"), sem("relu_done"), sem("hid_ready")
        hhi_ready, hlo_ready, down_done = sem("hhi_ready"), sem("hlo_ready"), sem("down_done")
        y_copied, yt_done, y_ready = sem("y_copied"), sem("yt_done"), sem("y_ready")
        stored = sems("stored", 2)

        gates_summed, gates_copied, gates_stored = sem("gates_summed"), sem("gates_copied"), sem("gates_stored")
        far_in = sems("far_in", (BLOCKS - NEAR) // FAR_CUT)
        gate_rest, identb_ready = sem("gate_rest"), sem("identb_ready")
        GATE_STEPS = 12

        def after(eng, semaphore, n):
            if not (isinstance(n, int) and n <= 0):
                eng.wait_ge(semaphore, n)

        def batch(t):
            return 0 <= t < B if isinstance(t, int) else True

        def group(i):
            return 0 <= i < GROUPS if isinstance(i, int) else True

        def steps(eng, step, extra, early=lambda t: None):
            def peeled(first, last):
                for t in range(first, last):
                    step(t, t % 2, lambda d: (t + d) // 2 + 1)
                    extra(t)

            def looped(first, last, also):
                with eng.Fori(first, last) as i:
                    for j in range(UNROLL):
                        step(i * UNROLL + j, j % 2, lambda d: i * (UNROLL // 2) + ((j + d) // 2 + 1))
                        also(i * UNROLL + j)

            peeled(-2, UNROLL)
            looped(1, MID, early)
            peeled(MID * UNROLL, (MID + 1) * UNROLL)
            looped(MID + 1, B // UNROLL - 1, lambda t: None)
            peeled(B - UNROLL, B + 2)

        def bodies(eng, body):
            for i in range(3):
                body(i, i % 2)
            with eng.Fori(1, GROUPS // 2 - 1) as k:
                body(k * 2 + 1, 1)
                body(k * 2 + 2, 0)
            body(GROUPS - 1, 1)

        block = stack.enter_context(nc.Block())

        @block.sync
        def _(sp):
            sp.dma_start(x_all[:, 0:X_CUTS[1], :], x[:, 0:X_CUTS[1], :]).then_inc(x_in[0], 16)
            for dst, src in ((ident, ident_c), (wq_sb, wq), (wk_sb, wk), (wv_sb, wv), (wo_sb, wo),
                             (remmask, remmask_c), (headmask, headmask_c)):
                sp.dma_start(dst[:], src).then_inc(weights_in, 16)
            column = lambda v: v.rearrange("(d a) -> d a", a=1)
            everywhere = lambda v, m: v.rearrange("(a d) -> a d", a=1).broadcast_to([P, m])
            sp.dma_start(bias_q[:], column(bq)).then_inc(small_in, 16)
            sp.dma_start(bias_k[:], column(bk)).then_inc(small_in, 16)
            sp.dma_start(bv_rows[:], everywhere(bv, D)).then_inc(small_in, 16)
            sp.dma_start(bo_rows[:], everywhere(bo, D)).then_inc(small_in, 16)
            sp.dma_start(gates_in[:, 0:1], everywhere(g_xattn, 1)).then_inc(small_in, 16)
            sp.dma_start(gates_in[:, 1:2], everywhere(g_ffn, 1)).then_inc(small_in, 16)
            def load(t, p):
                row = bass.ds(t, 1)
                after(sp, proj_done, t - 1)
                sp.dma_start(ctxT[:, p, :], ctx_in[row].rearrange("o d k -> (o d) k")).then_inc(ctx_ld[p], 16)
                after(sp, negm_ready, t - 1)
                sp.dma_start(mask_in[:, p, :], mask[row].rearrange("o s k -> (o s) k")).then_inc(mask_ld[p], 16)
                after(sp, w_ready[1], t - 1)
                sp.dma_start(prob_g[:, p, :], fside[row].rearrange("o s k -> (o s) k")).then_inc(g_ld[p], 16)

            load(0, 0)
            load(1, 1)
            load(2, 0)
            load(3, 1)
            with sp.Fori(1, B // UNROLL) as i:
                for j in range(UNROLL):
                    load(i * UNROLL + j, j % 2)

            outr = out.rearrange("(g j) s d -> s g j d", j=TILES)

            def spread(i):
                sp.wait_ge(gates_copied, i + 1)
                after(sp, hid_ready, i * BLOCKS)
                sp.dma_start(gates_dram, gates_all[:]).then_inc(gates_stored, 16)
                sp.wait_ge(gates_stored, (i + 1) * 16)
                by_half = gates_dram.rearrange("(f h) n -> h f n", h=2)
                for c in range((BLOCKS - NEAR) // FAR_CUT):
                    for h in range(2):
                        f = NEAR + c * FAR_CUT
                        src = by_half[h:h + 1, f:f + FAR_CUT, :].broadcast_to([FE, FAR_CUT, GT])
                        sp.dma_start(gates_far[h * FE:(h + 1) * FE, c * FAR_CUT:(c + 1) * FAR_CUT, :], src).then_inc(far_in[c], 16)

            def store(i, p):
                sp.wait_ge(y_ready, i + 1)
                sp.dma_start(outr[:, bass.ds(i, 1)].rearrange("s g j d -> s (g j) d"), y_out[:, p]).then_inc(stored[p], 16)

            spread(0)
            with sp.Fori(0, GROUPS // 2 - 1) as k:
                spread(k * 2 + 1)
                store(k * 2, 0)
                spread(k * 2 + 2)
                store(k * 2 + 1, 1)
            spread(GROUPS - 1)
            store(GROUPS - 2, 0)
            store(GROUPS - 1, 1)
            for p in range(2):
                sp.wait_ge(stored[p], 16 * (GROUPS // 2))

        @block.tensor
        def _(pe):
            def warm(n):
                for _ in range(n):
                    pe.matmul(ps[:, bank_o, 0:2 * P], zeros[:, 0:P], zeros[:], start=True, stop=True)

            pe.wait_ge(zeros_ready, 1)
            warm(12)
            pe.wait_ge(weights_in, 16 * 7)

            def step(t, p, used):
                q = 1 - p
                if batch(t):
                    pe.wait_ge(q_ready, t + 1)
                    pe.wait_ge(kblk_ready, t + 1)

                def logits(r):
                    if r >= 2:
                        pe.wait_ge(lg_masked[r - 2], t + 1)
                    else:
                        after(pe, lg_masked[r + 2], t)
                    rows = slice(32 * r, 32 * r + 32)
                    pe.matmul(ps[:, bank_lg[r % 2], 0:4 * KEYS], qT[rows, p, :],
                              kblk[rows, p].rearrange("p a b -> p (a b)"),
                              start=True, stop=True).then_inc(lg_done[r], 1)

                def turn(n, u):
                    pe.wait_ge(w_ready[0], u + 1)
                    if n > 0:
                        pe.wait_ge(w_ready[1], u + 1)
                    after(pe, pt_copied[n], u)
                    for c, (kind, m) in enumerate(SETS[n]):
                        src = wrem[:, q, m, :] if kind == "rem" else \
                            wmain[:, q, 2 * m:2 * m + 2, :].rearrange("p a b -> p (a b)")
                        last = pe.transpose(ps[:, bank_pt[n], c * P:(c + 1) * P], src, ident[:])
                    last.then_inc(pt_done[n], 1)

                def heads(u, sets):
                    for n in sets:
                        pe.wait_ge(pt_copied[n], u + 1)
                        for c, (kind, m) in enumerate(SETS[n]):
                            lhsT = vrem[:, p, m * P:(m + 1) * P] if kind == "rem" else vmain[:, p, m * P:(m + 1) * P]
                            last = pe.matmul(ps[:, bank_o, 0:P], lhsT, wT[:, p, 4 * n + c, :],
                                             start=(n == 0 and c == 0), stop=(4 * n + c == len(CHUNKS) - 1))
                    if n == len(SETS) - 1:
                        last.then_inc(pv_done, 1)

                if batch(t):
                    logits(0)
                    logits(1)
                if batch(t + 1):
                    pe.wait_ge(ct_copied, t + 2)
                    pe.wait_ge(ctx_ld[q], used(1) * 16)
                    after(pe, v_copied, t + 1)
                    o = ps[:, bank_proj, :]
                    pe.matmul(o[:, 0:P], wq_sb[:], ct[:, q, 0:P], start=True, stop=True)
                    pe.matmul(o[:, P:P + KEYS], wk_sb[:], ctxT[:, q, KMAIN:KMAIN + KEYS], start=True, stop=True)
                    pe.matmul(o[:, P + KEYS:2 * P + KEYS], ctxT[:, q, 0:P], wv_sb[:], start=True, stop=True)
                    pe.matmul(o[:, 2 * P + KEYS:3 * P + KEYS], ctxT[:, q, P:2 * P], wv_sb[:],
                              start=True, stop=True).then_inc(proj_done, 1)
                after(pe, ct_copied, t + 2)
                if batch(t + 2):
                    pe.wait_ge(xn_ready, t + 3)
                    last = pe.transpose(ps[:, bank_ct, 0:P], xn[:, p, :], ident[:])
                if batch(t - 2):
                    pe.wait_ge(rexp_ready, t - 1)
                    last = pe.transpose(ps[:, bank_ct, P:2 * P], rexp[:].rearrange("p h d -> p (h d)"), ident[:])
                last.then_inc(ct_done, 1)
                if batch(t - 2):
                    pe.wait_ge(vmain_ready, t - 1)
                    pe.wait_ge(vrem_ready, t - 1)
                    after(pe, x1_ready, t - 2)
                    heads(t - 2, [0])
                if batch(t):
                    logits(2)
                    logits(3)
                if batch(t - 2):
                    heads(t - 2, [1, 2])
                if batch(t - 1):
                    turn(0, t - 1)
                    turn(1, t - 1)
                    turn(2, t - 1)
                if batch(t - 2):
                    pe.wait_ge(oT_ready, t - 1)
                    pe.wait_ge(gated_w, 3)
                    pe.matmul(ps[:, bank_o, 2 * P:3 * P], oT[:], wo_g[:], start=True, stop=True).then_inc(r_done, 1)

            def turn_x(i):
                pe.wait_ge(x2_ready, i + 1)
                if isinstance(i, int) and i == 0:
                    pe.wait_ge(v_copied, B)
                after(pe, gates_copied, i)
                for j in range(TILES):
                    last = pe.transpose(ps[:, bank_xy, j * P:(j + 1) * P], x2[:, j, :], ident[:])
                last.then_inc(xt_done, 1)

            def select(i, p):
                pe.wait_ge(xhi_ready, i + 1)
                pe.wait_ge(xlo_ready, i + 1)
                if isinstance(i, int) and i == 0:
                    pe.wait_ge(sel_split, 2)
                    pe.wait_ge(lg_masked[2], B)
                after(pe, gt_ready, i)
                for j in range(TILES):
                    o = ps[:, bank_sg, j * EXPERTS:(j + 1) * EXPERTS]
                    hi, lo = x2_hi[:, p, j * P:(j + 1) * P], x2_lo[:, p, j * P:(j + 1) * P]
                    pe.matmul(o, hi, sel_hi[:], start=True, stop=False)
                    pe.matmul(o, hi, sel_lo[:], start=False, stop=False)
                    last = pe.matmul(o, lo, sel_hi[:], start=False, stop=True)
                last.then_inc(sel_done, 1)

            def turn_g(i):
                pe.wait_ge(gparts_ready, i + 1)
                if isinstance(i, int) and i == 0:
                    pe.wait_ge(identb_ready, 1)
                pe.wait_ge(egate_ready, i + 1)
                o = ps[0:96, bank_sg, 0:GT // 2].bitcast(BF16)
                for j in range(TILES):
                    last = pe.transpose(o[:, j * P:(j + 1) * P], gparts[:, j].rearrange("p a e -> p (a e)"),
                                        identb[:])
                last.then_inc(gt_done, 1)

            def up(i, f, p):
                n = i * BLOCKS + f
                if isinstance(i, int) and i == 0 and f == 0:
                    pe.wait_ge(lg_masked[3], B)
                    pe.wait_ge(ct_copied, B + 4)
                    for r in range(2):
                        pe.wait_ge(pt_copied[r], B)
                    pe.wait_ge(keys_split, 2 * BLOCKS)
                    pe.wait_ge(late_in, 16 * 2)
                after(pe, relu_done, n - 1)
                w = slice(f * P, (f + 1) * P)
                o = ps[:, bank_u[f % 2], :]
                pe.matmul(o, keys_hi[:, w], x2_hi[:, p, :], start=True, stop=False)
                pe.matmul(o, keys_hi[:, w], x2_lo[:, p, :], start=False, stop=False)
                pe.matmul(o, keys_lo[:, w], x2_hi[:, p, :], start=False, stop=True).then_inc(u_done, 1)
                if f >= NEAR:
                    return
                after(pe, hid_ready, n - 1 if f > 1 else n - BLOCKS + NEAR - 1)
                pe.matmul(ps[:, bank_g[f % 2], :], gatesel[:, 2 * f:2 * f + 2, :].rearrange("p e f -> p (e f)").bitcast(BF16),
                          gT[:, p, :], start=True, stop=True).then_inc(gb_done, 1)

            def down(i, f, p):
                n = i * BLOCKS + f
                pe.wait_ge(hhi_ready, n + 1)
                pe.wait_ge(hlo_ready, n + 1)
                w, s = slice(f * P, (f + 1) * P), f % LAG
                if f == 0:
                    after(pe, y_copied, i - 1)
                    if isinstance(i, int) and i == 0:
                        pe.wait_ge(pt_copied[2], B)
                    if isinstance(i, int) and i == 1:
                        pe.wait_ge(x1_ready, B)
                o = ps[:, bank_y[p], :]
                pe.matmul(o, values_hi[:, w], hid_hi[:, s, :], start=(f == 0), stop=False)
                pe.matmul(o, values_lo[:, w], hid_hi[:, s, :], start=False, stop=False)
                pe.matmul(o, values_hi[:, w], hid_lo[:, s, :], start=False, stop=(f == BLOCKS - 1)).then_inc(down_done, 1)

            def sum_gates(i, p):
                if isinstance(i, int) and i == 0:
                    pe.wait_ge(xlo_ready, 1)
                after(pe, y_ready, i - 1)
                pe.matmul(ps[0:EXPERTS, bank_xy, :], gatesel[:, :, 0].bitcast(BF16), gT[:, p, :],
                          start=True, stop=True).then_inc(gates_summed, 1)

            def turn_y(i):
                pe.wait_ge(y_copied, i + 1)
                pe.wait_ge(xlo_ready, min(i + 3, GROUPS) if isinstance(i, int) else i + 3)
                after(pe, y_ready, i)
                for j in range(TILES):
                    last = pe.transpose(ps[:, bank_xy, j * P:(j + 1) * P], yT[:, j * P:(j + 1) * P], ident[:])
                last.then_inc(yt_done, 1)

            def body(i, p):
                pe.wait_ge(gt_ready, i + 1)
                for f in range(BLOCKS):
                    up(i, f, p)
                    if f >= LAG:
                        down(i, f - LAG, p)
                    elif group(i - 1):
                        down(i - 1, BLOCKS + f - LAG, 1 - p)
                    if f == 8 and group(i - 1):
                        turn_y(i - 1)
                    if f == 0:
                        sum_gates(i, p)
                    if group(i + 1):
                        if f == 2:
                            turn_x(i + 1)
                        if f == 5:
                            select(i + 1, 1 - p)
                        if f == 13:
                            turn_g(i + 1)

            def extra(t):
                if t == -2:
                    warm(4)
                if t == -1:
                    warm(2)
                if t == 0:
                    warm(2)
                if t == B - 2:
                    turn_x(0)
                if t == B - 1:
                    select(0, 0)
                if t == B + 1:
                    turn_g(0)

            steps(pe, step, extra)
            bodies(pe, body)
            for f in range(BLOCKS - LAG, BLOCKS):
                down(GROUPS - 1, f, 1)
            turn_y(GROUPS - 1)

        @block.scalar
        def _(act):
            def root(n, first, last):
                act.wait_ge(var_ready[n], 7)
                act.activation(norm_tmp[:, 5, first:last], norm_tmp[:, 4, first:last], ACT.Sqrt).then_inc(root_done[n], 1)

            root(0, X_CUTS[0], X_CUTS[1])
            def load_x(c):
                cut = slice(X_CUTS[c], X_CUTS[c + 1])
                act.dma_start(x_all[:, cut, :], x[:, cut, :]).then_inc(x_in[c], 16)

            act.wait_ge(small_in, 16 * 6)
            load_x(1)
            act.activation(gates_tanh[:], gates_in[:], ACT.Tanh).then_inc(tanh_done, 1)
            act.activation(bias_qs[:], bias_q[:], ACT.Copy, scale=DH ** -0.5).then_inc(tanh_done, 1)
            act.wait_ge(tanh_done, 2)

            def step(t, p, used):
                q = 1 - p

                def copy_set(n, u):
                    act.wait_ge(pt_done[n], u + 1)
                    after(act, pv_done, u - 1)
                    w = len(SETS[n]) * P
                    act.copy(wT[:, q, 4 * n:4 * n + len(SETS[n]), :].rearrange("p c k -> p (c k)"),
                             ps[:, bank_pt[n], 0:w]).then_inc(pt_copied[n], 1)

                def exponentials(first, last):
                    for h in range(first, last):
                        v = act.activation(soft[:, p, h, :], soft[:, p, h, :], ACT.Exp,
                                           bias=negmax[:, p, h:h + 1], accum_out=sums[:, p, h:h + 1])
                    v.then_inc(exp_done[0], 1)

                if batch(t + 1):
                    act.wait_ge(proj_done, t + 2)
                    after(act, kblk_ready, t)
                    act.activation(kv[:, q, 0:KEYS], ps[:, bank_proj, P:P + KEYS], ACT.Identity,
                                   bias=bias_k[:, 0:1]).then_inc(k_copied, 1)
                    after(act, lg_done[3], t)
                    act.activation(qT[:, q, :], ps[:, bank_proj, 0:P], ACT.Identity, scale=DH ** -0.5,
                                   bias=bias_qs[:, 0:1]).then_inc(q_ready, 1)
                    after(act, vmain_ready, t)
                    after(act, vremm_ready, t)
                    act.copy(kv[:, q, KEYS:], ps[:, bank_proj, P + KEYS:P + KEYS + 2 * P]).then_inc(v_copied, 1)
                act.wait_ge(ct_done, t + 3)
                after(act, proj_done, min(t + 1, B) if isinstance(t, int) else t + 1)
                after(act, oT_ready, t - 3)
                cols = slice(0 if batch(t + 2) else P, 2 * P if batch(t - 2) else P)
                act.copy(ct[:, p, cols], ps[:, bank_ct, cols]).then_inc(ct_copied, 1)
                if batch(t):
                    act.wait_ge(max_ready[0], t + 1)
                    after(act, rsum_ready, t - 1)
                    exponentials(0, HALF)
                if batch(t):
                    act.wait_ge(shifted, t + 1)
                    o = soft[:, p, HALF:H, :].rearrange("p h k -> p (h k)")
                    act.activation(o, o, ACT.Exp).then_inc(exp_done[1], 1)
                if batch(t - 1):
                    act.wait_ge(rsum_ready, t)
                    after(act, ct_done, t + 3)
                    act.copy(rexp[:], rsum[:, q, :, None].broadcast_to([P, H, DH])).then_inc(rexp_ready, 1)
                    for n in range(3):
                        copy_set(n, t - 1)

            def copy_x(i, p):
                act.wait_ge(xt_done, i + 1)
                after(act, u_done, (i - 1) * BLOCKS + 1)
                act.copy(x2_hi[:, p, :], ps[:, bank_xy, :]).then_inc(xhi_ready, 1)

            def gate_exp(i):
                act.wait_ge(sel_done, i + 1)
                after(act, gate_steps, (i - 1) * GATE_STEPS + 1)
                act.activation(egate[:].rearrange("p j e -> p (j e)"), ps[:, bank_sg, 0:TILES * EXPERTS],
                               ACT.Exp, scale=neg_unscale_sel[:, 0:1]).then_inc(egate_ready, 1)

            def copy_g(i, p):
                act.wait_ge(gt_done, i + 1)
                after(act, gb_done, i * NEAR)
                act.copy(gT[:, p, :], ps[0:96, bank_sg, 0:GT // 2].bitcast(BF16)).then_inc(gt_ready, 1)

            def copy_gates(i):
                act.wait_ge(gates_summed, i + 1)
                after(act, gates_stored, i * 16)
                act.copy(gates_all[:], ps[0:EXPERTS, bank_xy, :]).then_inc(gates_copied, 1)

            def relu(i, f):
                n = i * BLOCKS + f
                act.wait_ge(u_done, n + 1)
                after(act, hid_ready, n - 1)
                act.activation(relu_u[:, f % 2, :], ps[:, bank_u[f % 2], :], ACT.Relu).then_inc(relu_done, 1)

            def high(i, f):
                n = i * BLOCKS + f
                act.wait_ge(hid_ready, n + 1)
                after(act, down_done, n - LAG + 1)
                act.copy(hid_hi[:, f % LAG, :], hid[:, f % LAG, :]).then_inc(hhi_ready, 1)

            def copy_y(i, p):
                act.wait_ge(down_done, (i + 1) * BLOCKS)
                after(act, yt_done, i)
                act.activation(yT[:], ps[:, bank_y[p], :], ACT.Copy, scale=y_scale[:, 1:2]).then_inc(y_copied, 1)

            def body(i, p):
                for f in range(BLOCKS):
                    relu(i, f)
                    if f > 0:
                        high(i, f - 1)
                    elif group(i - 1):
                        high(i - 1, BLOCKS - 1)
                    if f == 5 and group(i - 1):
                        copy_y(i - 1, 1 - p)
                    if f == 1:
                        copy_gates(i)
                    if isinstance(i, int) and i == 0 and f == 4:
                        root(3, FIRST, B)
                    if group(i + 1):
                        if f == 3:
                            copy_x(i + 1, 1 - p)
                        if f == 6:
                            gate_exp(i + 1)
                        if f == 14:
                            copy_g(i + 1, 1 - p)

            def extra(t):
                if t == -1:
                    load_x(2)
                if t == 0:
                    act.dma_start(keys_raw[:], keys).then_inc(keys_in, 16)
                if t == 1:
                    act.dma_start(values_raw[:], values).then_inc(values_in, 16)
                    act.dma_start(selT[:], expert_sel).then_inc(values_in, 16)
                if t == 2:
                    load_x(3)
                    root(1, X_CUTS[1], EARLY)
                if t == 3:
                    act.dma_start(restart[:], restart_c).then_inc(late_in, 16)
                    act.dma_start(gatesel[:].rearrange("p e f -> p (e f)"), gatesel_c).then_inc(late_in, 16)
                if t == MID * UNROLL:
                    root(4, EARLY, B)
                    root(2, 0, FIRST)
                if t == B - 2:
                    copy_x(0, 0)
                if t == B - 1:
                    act.wait_ge(unscale_ready, 2)
                    act.wait_ge(yscale_ready, 2)
                    gate_exp(0)
                if t == B + 1:
                    copy_g(0, 0)

            steps(act, step, extra)
            bodies(act, body)
            high(GROUPS - 1, BLOCKS - 1)
            copy_y(GROUPS - 1, 1)

        @block.vector
        def _(dve):
            dve.memset(zeros[:], 0.0).then_inc(zeros_ready, 1)
            dve.memset(wrem[:], 0.0).then_inc(zeroed, 1)
            def token_stats(first, last):
                for b in range(first, last):
                    dve.bn_stats(bn1[:, b, :], x_all[:, b, :]).then_inc(bn1_ready, 1)

            def late_stats(b):
                row = bass.ds(b, 1)
                dve.bn_stats(bn1[:, row, :].rearrange("p o d -> p (o d)"),
                             x_all[:, row, :].rearrange("p o d -> p (o d)")).then_inc(bn1_ready, 1)

            def variance(n, bn, mean, first, last):
                cut, done = slice(first, last), var_ready[n]
                mean_sum, mean_diff, sq_sum, sq_diff, var_eps = (norm_tmp[:, k, cut] for k in range(5))
                me, qe, mo, qo = (bn[:, cut, k] for k in (1, 2, 4, 5))
                dve.tensor_tensor(mean_sum, me, mo, ALU.add).then_inc(done, 1)
                dve.tensor_tensor(mean_diff, me, mo, ALU.subtract).then_inc(done, 1)
                dve.tensor_tensor(sq_sum, qe, qo, ALU.add).then_inc(done, 1)
                dve.wait_ge(done, 1)
                dve.tensor_scalar(mean[:, cut], mean_sum, 0.5, None, ALU.mult).then_inc(done, 1)
                dve.wait_ge(done, 2)
                dve.scalar_tensor_tensor(sq_diff, mean_diff, 0.25, mean_diff, ALU.mult, ALU.mult).then_inc(done, 1)
                dve.wait_ge(done, 5)
                dve.scalar_tensor_tensor(var_eps, sq_sum, 1.0 / D, sq_diff, ALU.mult, ALU.add).then_inc(done, 1)
                dve.wait_ge(done, 6)
                dve.tensor_scalar(var_eps, var_eps, EPS, None, ALU.add).then_inc(done, 1)

            def rstd(n, out, first, last):
                cut, ready = slice(first, last), rstd_ready[n]
                var_eps, root, y, z = (norm_tmp[:, k, cut] for k in range(4, 8))
                dve.wait_ge(root_done[n], 1)
                dve.reciprocal(y, root).then_inc(ready, 1)
                dve.wait_ge(ready, 1)
                dve.tensor_tensor(z, y, y, ALU.mult).then_inc(ready, 1)
                dve.wait_ge(ready, 2)
                dve.tensor_tensor(z, z, var_eps, ALU.mult).then_inc(ready, 1)
                dve.wait_ge(ready, 3)
                dve.tensor_scalar(z, z, -0.5, 1.5, ALU.mult, ALU.add).then_inc(ready, 1)
                dve.wait_ge(ready, 4)
                dve.tensor_tensor(out[:, cut], y, z, ALU.mult).then_inc(ready, 1)
                dve.wait_ge(ready, 5)

            dve.wait_ge(x_in[0], 16)
            token_stats(X_CUTS[0], X_CUTS[1])
            dve.wait_ge(bn1_ready, X_CUTS[1])
            variance(0, bn1, mean1, X_CUTS[0], X_CUTS[1])
            rstd(0, rstd1, X_CUTS[0], X_CUTS[1])
            dve.wait_ge(vzeroed, 2)

            def step(t, p, used):
                q = 1 - p

                def norm(u, up):
                    after(dve, ct_done, u - 1)
                    b = bass.ds(u, 1)
                    dve.tensor_scalar(xn[:, up, :], x_all[:, b, :].rearrange("p o d -> p (o d)"), mean1[:, b], rstd1[:, b],
                                      ALU.subtract, ALU.mult).then_inc(xn_ready, 1)

                def masked(r):
                    dve.wait_ge(lg_done[r], t + 1)
                    dve.tensor_tensor(soft[:, p, 4 * r:4 * r + 4, :],
                                      ps[:, bank_lg[r % 2], 0:4 * KEYS].rearrange("p (h k) -> p h k", h=4),
                                      negm[:, p, None, :].broadcast_to([P, 4, KEYS]), ALU.add).then_inc(lg_masked[r], 1)

                def negated_max(m):
                    dve.wait_ge(lg_masked[2 * m + 1], t + 1)
                    dve.tensor_reduce(negmax[:, p, HALF * m:HALF * m + HALF], soft[:, p, HALF * m:HALF * m + HALF, :],
                                      AX.X, ALU.max, negate=True).then_inc(max_ready[m], 1)

                if batch(t):
                    dve.wait_ge(negm_ready, t + 1)
                    after(dve, w_ready[1], t - 1)
                    masked(0)
                    masked(1)
                    after(dve, exp_done[0], t - 1)
                    negated_max(0)
                if batch(t - 1):
                    dve.wait_ge(exp_done[1], t)
                    dve.tensor_reduce(sums[:, q, HALF:H], soft[:, q, HALF:H, :], AX.X, ALU.add).then_inc(sumb_ready, 1)
                if batch(t):
                    masked(2)
                if batch(t - 1):
                    dve.wait_ge(sumb_ready, t)
                    dve.wait_ge(exp_done[0], t)
                    after(dve, rexp_ready, t - 2)
                    dve.reciprocal(rsum[:, q, :], sums[:, q, :]).then_inc(rsum_ready, 1)
                if isinstance(t, int) and t == -2:
                    norm(0, 0)
                if batch(t + 3):
                    norm(t + 3, q)
                if batch(t):
                    masked(3)
                    negated_max(1)
                if batch(t - 2):
                    dve.wait_ge(pv_done, t - 1)
                    dve.wait_ge(ct_copied, t + 3)
                    after(dve, r_done, t - 2)
                    dve.tensor_tensor(oT[:], ps[:, bank_o, 0:P], ct[:, p, P:2 * P], ALU.mult).then_inc(oT_ready, 1)
                if batch(t):
                    dve.wait_ge(max_ready[1], t + 1)
                    dve.tensor_tensor(soft[:, p, HALF:H, :], soft[:, p, HALF:H, :],
                                      negmax[:, p, HALF:H, None].broadcast_to([P, HALF, KEYS]), ALU.add).then_inc(shifted, 1)
                if batch(t - 2):
                    b = bass.ds(t - 2, 1)
                    dve.wait_ge(r_done, t - 1)
                    dve.wait_ge(xb_ready, t - 1)
                    dve.tensor_tensor(x_all[:, b, :].rearrange("p o d -> p (o d)"), ps[:, bank_o, 2 * P:3 * P], xb[:, p, :],
                                      ALU.add).then_inc(x1_ready, 1)
                    dve.wait_ge(x1_ready, t - 1)
                if batch(t):
                    after(dve, pv_done, t - 1)
                    dve.wait_ge(v_copied, t + 1)
                    for e in range(2):
                        rows = slice(KMAIN * e, KMAIN * e + KMAIN)
                        pairs = lambda v: v.rearrange("p (m e d) -> p m e d", e=2, d=DH)[:, :, e, :]
                        v = dve.tensor_tensor(vmain[rows, p, :].rearrange("p (m w) -> p m w", w=MAIN_STEP)[:, :, DH * e:DH * e + DH],
                                              pairs(kv[rows, p, KEYS:KEYS + P]), pairs(bv_rows[rows]), ALU.add)
                    v.then_inc(vmain_ready, 1)
                if batch(t - 2):
                    dve.bn_stats(bn2[:, b, :].rearrange("p o d -> p (o d)"),
                                 x_all[:, b, :].rearrange("p o d -> p (o d)")).then_inc(bn2_ready, 1)

            def magnitude(n, src):
                dve.tensor_reduce(magn[:, n:n + 1], src[:], AX.X, ALU.max,
                                  apply_absolute_value=True).then_inc(magn_ready, 1)

            def scales():
                dve.wait_ge(magn_shared, 1)
                dve.tensor_scalar(magn_exp[:], magn_all[:].bitcast(I32), EXP_MASK, None, ALU.bitwise_and).then_inc(exp_ready, 1)
                dve.wait_ge(exp_ready, 1)
                dve.tensor_scalar(magn_exp[:], magn_exp[:], float(LEAST_EXP << 23), None, ALU.max).then_inc(exp_ready, 1)
                dve.wait_ge(exp_ready, 2)
                dve.tensor_scalar(scale_w[:].bitcast(I32), magn_exp[:], -1.0, float((254 + SCALED_EXP) << 23),
                                  ALU.mult, ALU.add).then_inc(scale_ready, 1)
                dve.tensor_scalar(unscale_w[:].bitcast(I32), magn_exp[:], float(-(SCALED_EXP << 23)), None,
                                  ALU.add).then_inc(unscale_ready, 1)
                dve.wait_ge(scale_ready, 1)
                dve.tensor_scalar(sel_hi[:], selT[:], scale_w[:, 2:3], None, ALU.mult).then_inc(sel_split, 1)
                dve.wait_ge(sel_split, 1)
                dve.scalar_tensor_tensor(sel_lo[:], selT[:], scale_w[:, 2:3], sel_hi[:], ALU.mult, ALU.subtract).then_inc(sel_split, 1)
                dve.wait_ge(unscale_ready, 1)
                dve.tensor_scalar(neg_unscale_sel[:], unscale_w[:, 2:3], -1.0, None, ALU.mult).then_inc(unscale_ready, 1)
                dve.tensor_scalar(y_scale[:, 0:1], unscale_w[:, 0:1], unscale_w[:, 1:2], 1 / HIDDEN_SHIFT,
                                  ALU.mult, ALU.mult).then_inc(yscale_ready, 1)
                dve.wait_ge(yscale_ready, 1)
                dve.tensor_scalar(y_scale[:, 1:2], y_scale[:, 0:1], gates_tanh[:, 1:2], None, ALU.mult).then_inc(yscale_ready, 1)

            def normed(i):
                after(dve, xt_done, i)
                for j in range(TILES):
                    b = bass.ds(i * TILES + j, 1)
                    v = dve.tensor_scalar(x2[:, j, :], x_all[:, b, :].rearrange("p o d -> p (o d)"), mean2[:, b],
                                          rstd2[:, b], ALU.subtract, ALU.mult)
                v.then_inc(x2_ready, 1)

            def low_x(i, p):
                dve.wait_ge(xhi_ready, i + 1)
                after(dve, u_done, (i - 1) * BLOCKS + 1)
                dve.tensor_tensor(x2_lo[:, p, :], ps[:, bank_xy, :], x2_hi[:, p, :], ALU.subtract).then_inc(xlo_ready, 1)

            def chain(i, k):
                dve.wait_ge(gate_steps, i * GATE_STEPS + k)

            def gates(i):
                dve.wait_ge(egate_ready, i + 1)
                dve.tensor_scalar(dgate[:], egate[:], 1.0, None, ALU.add).then_inc(gate_steps, 1)
                chain(i, 1)
                dve.reciprocal(gate[:], dgate[:]).then_inc(gate_steps, 1)
                chain(i, 2)

            def gates_top(i):
                fourth = best[:, :, TOP - 1:TOP].broadcast_to([P, TILES, EXPERTS])
                for j in range(TILES):
                    v = dve.max(best[:, j, :], gate[:, j, :])
                v.then_inc(gate_steps, 1)
                chain(i, 3)
                dve.tensor_tensor(above[:], gate[:], fourth, ALU.is_gt).then_inc(gate_steps, 1)
                dve.tensor_tensor(equal[:], gate[:], fourth, ALU.is_equal).then_inc(gate_steps, 1)

            def gates_more(i):
                chain(i, 4)
                dve.tensor_reduce(n_above[:], above[:], AX.X, ALU.add).then_inc(gate_steps, 1)
                chain(i, 5)
                if isinstance(i, int) and i == 0:
                    dve.wait_ge(late_in, 16 * 2)
                dve.tensor_tensor_scan(rank[:].rearrange("p j e -> p (j e)"), restart[:],
                                       equal[:].rearrange("p j e -> p (j e)"), 0.0, ALU.mult, ALU.add).then_inc(gate_steps, 1)
                chain(i, 7)
                dve.tensor_tensor(rank2[:], rank[:], n_above[:, :, None].broadcast_to([P, TILES, EXPERTS]),
                                  ALU.add).then_inc(gate_steps, 1)

            def gates_kept(i):
                chain(i, 8)
                dve.scalar_tensor_tensor(taken[:], rank2[:], float(TOP), equal[:], ALU.is_le, ALU.mult).then_inc(gate_steps, 1)
                chain(i, 9)
                dve.tensor_tensor(kept[:], taken[:], above[:], ALU.add).then_inc(gate_steps, 1)
                chain(i, 10)
                after(dve, gt_done, i)
                dve.tensor_tensor(gsel[:], kept[:], gate[:], ALU.mult).then_inc(gate_steps, 1)

            def split_gates(i):
                chain(i, 11)
                dve.tensor_copy(gparts[:, :, 0, :], gsel[:]).then_inc(gate_steps, 1)
                chain(i, 12)
                dve.tensor_tensor(grest1[:], gsel[:], gparts[:, :, 0, :], ALU.subtract).then_inc(gate_rest, 1)

            def split_more(i):
                dve.wait_ge(gate_rest, i * 3 + 1)
                dve.tensor_copy(gparts[:, :, 1, :], grest1[:]).then_inc(gate_rest, 1)
                dve.wait_ge(gate_rest, i * 3 + 2)
                dve.tensor_tensor(grest2[:], grest1[:], gparts[:, :, 1, :], ALU.subtract).then_inc(gate_rest, 1)
                dve.wait_ge(gate_rest, i * 3 + 3)
                dve.tensor_copy(gparts[:, :, 2, :], grest2[:]).then_inc(gparts_ready, 1)

            def hidden(i, f):
                n = i * BLOCKS + f
                dve.wait_ge(relu_done, n + 1)
                if f < NEAR:
                    dve.wait_ge(gb_done, i * NEAR + (f + 1))
                    g = ps[:, bank_g[f % 2], :]
                else:
                    dve.wait_ge(far_in[(f - NEAR) // FAR_CUT], (i + 1) * 32)
                    g = gates_far[:, f - NEAR, :]
                after(dve, hlo_ready, n - LAG + 1)
                dve.tensor_tensor(hid[:, f % LAG, :], relu_u[:, f % 2, :], g, ALU.mult).then_inc(hid_ready, 1)

            def residual(i, p, uses):
                dve.wait_ge(yt_done, i + 1)
                after(dve, stored[p], uses * 16)
                dve.tensor_tensor(y_out[:, p], ps[:, bank_xy, :].rearrange("p (j d) -> p j d", j=TILES),
                                  x_all[:, bass.ds(i * TILES, TILES), :], ALU.add).then_inc(y_ready, 1)

            def body(i, p, uses):
                for f in range(BLOCKS):
                    hidden(i, f)
                    if f == 12 and group(i - 1):
                        residual(i - 1, 1 - p, uses)
                    if isinstance(i, int) and i == 0 and f == 1:
                        dve.wait_ge(bn2_ready, B)
                        variance(3, bn2, mean2, FIRST, B)
                    if isinstance(i, int) and i == 0 and f == 5:
                        rstd(3, rstd2, FIRST, B)
                    if group(i + 1):
                        if f == 0:
                            normed(i + 1)
                        if f == 3:
                            low_x(i + 1, 1 - p)
                        if f == 6:
                            gates(i + 1)
                        if f == 7:
                            gates_top(i + 1)
                        if f == 8:
                            gates_more(i + 1)
                        if f == 9:
                            gates_kept(i + 1)
                        if f == 10:
                            split_gates(i + 1)
                        if f == 11:
                            split_more(i + 1)

            def extra(t):
                if t == -1:
                    dve.wait_ge(weights_in, 16 * 7)
                    dve.wait_ge(small_in, 16 * 6)
                    dve.wait_ge(tanh_done, 1)
                    dve.tensor_scalar(wo_g[:], wo_sb[:], gates_tanh[:, 0:1], None, ALU.mult).then_inc(gated_w, 1)
                    dve.tensor_scalar(bo_g[:], bo_rows[:], gates_tanh[:, 0:1], None, ALU.mult).then_inc(gated_w, 1)
                    dve.tensor_tensor(bv_rem[:], bv_rows[:], remmask[:], ALU.mult).then_inc(gated_w, 1)
                    dve.wait_ge(x_in[1], 16)
                    token_stats(8, 16)
                if t == 0:
                    dve.wait_ge(x_in[2], 16)
                    token_stats(16, 24)
                if t == 1:
                    token_stats(24, 32)
                    dve.wait_ge(keys_in, 16)
                    magnitude(0, keys_raw)
                if t == 2:
                    token_stats(32, EARLY)
                    dve.wait_ge(bn1_ready, EARLY)
                    variance(1, bn1, mean1, X_CUTS[1], EARLY)
                    dve.wait_ge(values_in, 16 * 2)
                    magnitude(1, values_raw)
                    magnitude(2, selT)
                if t == 3:
                    rstd(1, rstd1, X_CUTS[1], EARLY)
                    scales()
                    dve.wait_ge(x_in[3], 16)
                if t == MID * UNROLL:
                    dve.wait_ge(bn1_ready, B)
                    variance(4, bn1, mean1, EARLY, B)
                    dve.wait_ge(bn2_ready, FIRST)
                    variance(2, bn2, mean2, 0, FIRST)
                if t == MID * UNROLL + 1:
                    rstd(4, rstd1, EARLY, B)
                if t == MID * UNROLL + 2:
                    rstd(2, rstd2, 0, FIRST)
                if t == B - 3:
                    normed(0)
                if t == B - 2:
                    low_x(0, 0)
                if t == B - 1:
                    gates(0)
                    gates_top(0)
                if t == B:
                    gates_more(0)
                    gates_kept(0)
                    split_gates(0)
                    split_more(0)

            steps(dve, step, extra, lambda t: late_stats(t + (EARLY - UNROLL)))
            body(0, 0, 0)
            body(1, 1, 0)
            body(2, 0, 0)
            with dve.Fori(1, GROUPS // 2 - 1) as k:
                body(k * 2 + 1, 1, k)
                body(k * 2 + 2, 0, k)
            body(GROUPS - 1, 1, GROUPS // 2 - 1)
            residual(GROUPS - 1, 1, GROUPS // 2 - 1)

        @block.gpsimd
        def _(pool):
            pool.memset(vmain[:], 0.0).then_inc(vzeroed, 1)
            pool.memset(vrem[:], 0.0).then_inc(vzeroed, 1)
            pool.wait_ge(vzeroed, 2)
            pool.wait_ge(zeroed, 1)
            pool.wait_ge(weights_in, 16 * 7)
            pool.tensor_copy(identb[:], ident[:]).then_inc(identb_ready, 1)
            pool.wait_ge(gated_w, 3)

            def step(t, p, used):
                q = 1 - p

                def weights(m, u, up, uses):
                    hs = slice(HALF * m, HALF * m + HALF)
                    pool.wait_ge(exp_done[m], u + 1)
                    pool.wait_ge(g_ld[up], uses * 16)
                    after(pool, pt_done[2], u - 1)
                    pool.tensor_tensor(wmain[:, up, hs, :], soft[:, up, hs, 0:KMAIN],
                                       prob_g[:, up, None, 0:KMAIN].broadcast_to([P, HALF, KMAIN]), ALU.mult)
                    pool.tensor_tensor(wrem[:, up, m, 0:HALF * KREM].rearrange("p (h k) -> p h k", h=HALF),
                                       soft[:, up, hs, KMAIN:KEYS],
                                       prob_g[:, up, None, KMAIN:KEYS].broadcast_to([P, HALF, KREM]), ALU.mult).then_inc(w_ready[m], 1)

                if batch(t + 1):
                    pool.wait_ge(mask_ld[q], used(1) * 16)
                    after(pool, lg_masked[3], t)
                if batch(t - 1):
                    weights(1, t - 1, q, used(-1))
                if batch(t + 1):
                    pool.tensor_scalar(negm[:, q, :], mask_in[:, q, :], -1.0, 1e9, ALU.add, ALU.mult).then_inc(negm_ready, 1)
                    pool.wait_ge(k_copied, t + 2)
                    after(pool, lg_done[3], t)
                    pool.tensor_tensor(kblk[:, q], kv[:, q, None, 0:KEYS].broadcast_to([P, 4, KEYS]),
                                       headmask[:, :, None].broadcast_to([P, 4, KEYS]), ALU.mult).then_inc(kblk_ready, 1)
                if batch(t):
                    pool.wait_ge(v_copied, t + 1)
                    after(pool, vrem_ready, t - 1)
                    pool.tensor_tensor(vrem_m[:, p, :], kv[:, p, KEYS + P:KEYS + 2 * P], remmask[:], ALU.mult).then_inc(vremm_ready, 1)
                if batch(t - 2):
                    after(pool, x1_ready, t - 3)
                    pool.tensor_tensor(xb[:, p, :], x_all[:, bass.ds(t - 2, 1), :].rearrange("p o d -> p (o d)"), bo_g[:],
                                       ALU.add).then_inc(xb_ready, 1)
                if batch(t):
                    pool.wait_ge(vremm_ready, t + 1)
                    after(pool, pv_done, t - 1)
                    halves = lambda v: v.rearrange("p (m w) -> p m w", m=2)
                    pool.tensor_tensor(halves(vrem[:, p, :])[:, :, 0:HALF * DH], halves(vrem_m[:, p, :]), halves(bv_rem[:]),
                                       ALU.add).then_inc(vrem_ready, 1)
                    weights(0, t, p, used(0))

            def split_part(i, cut, part):
                n = part // 2
                src, hi, lo = ((keys_raw, keys_hi, keys_lo), (values_raw, values_hi, values_lo))[n]
                if part % 2 == 0:
                    scale = scale_w[:, n:n + 1].broadcast_to([P, P])
                    pool.tensor_tensor(hi[:, cut], src[:, cut], scale, ALU.mult)
                    pool.tensor_tensor(scaled[:, n, :], src[:, cut], scale, ALU.mult).then_inc(scaled_ready, 1)
                else:
                    pool.wait_ge(scaled_ready, i * 2 + (n + 1))
                    pool.tensor_tensor(lo[:, cut], scaled[:, n, :], hi[:, cut], ALU.subtract).then_inc(keys_split, 1)

            def body(i, p):
                for f in range(BLOCKS):
                    n = i * BLOCKS + f
                    pool.wait_ge(hid_ready, n + 1)
                    pool.wait_ge(hhi_ready, n + 1)
                    after(pool, down_done, n - LAG + 1)
                    pool.tensor_tensor(hid_lo[:, f % LAG, :], hid[:, f % LAG, :], hid_hi[:, f % LAG, :],
                                       ALU.subtract).then_inc(hlo_ready, 1)

            def extra(t):
                if t == 2:
                    pool.wait_ge(magn_ready, 3)
                    pool.partition_all_reduce(magn_all[:], magn[:], P, ABSMAX).then_inc(magn_shared, 1)
                if t == 3:
                    pool.wait_ge(scale_ready, 1)

            for t in range(-2, UNROLL):
                step(t, t % 2, lambda d: (t + d) // 2 + 1)
                extra(t)
            for part in range(4):
                split_part(0, slice(0, P), part)
            with pool.Fori(1, B // UNROLL - 1) as i:
                for j in range(UNROLL):
                    step(i * UNROLL + j, j % 2, lambda d: i * (UNROLL // 2) + ((j + d) // 2 + 1))
                    split_part(i, bass.ds(i * P, P), j)
            for t in range(B - UNROLL, B + 2):
                step(t, t % 2, lambda d: (t + d) // 2 + 1)
                if t < B:
                    split_part(BLOCKS - 1, slice((BLOCKS - 1) * P, BLOCKS * P), t % UNROLL)
            bodies(pool, body)


_INS = ["x", "ctx_1024", "fside_BxSxS2_0", "mask_BxSxS2_ik1", "g_xattn", "g_ffn",
        "L0_xattn_wq_k", "L0_xattn_wq_b", "L0_xattn_wk_k", "L0_xattn_wk_b", "L0_xattn_wv_k", "L0_xattn_wv_b",
        "L0_xattn_wo_k", "L0_xattn_wo_b", "L0_ffn_expert_sel", "L0_ffn_keys", "L0_ffn_values"]


def shape_constants():
    part, col = np.arange(P)[:, None], np.arange(P)[None, :]
    headmask = (part % 32 // DH == np.arange(4)[None, :]).astype(np.float32)
    remmask = (part // KREM == col // DH % HALF).astype(np.float32)
    own = np.arange(96)[:, None] % EXPERTS == np.arange(EXPERTS * FE)[None, :] // FE
    gatesel = ((own * HIDDEN_SHIFT).astype(np.float32).view(np.uint32) >> 16).astype(np.uint16)
    restart = np.broadcast_to((col % EXPERTS != 0), (P, P)).astype(np.float32)
    return {"c_ident": np.eye(P, dtype=np.float32), "c_headmask": headmask, "c_remmask": remmask,
            "c_gatesel": gatesel, "c_restart": np.ascontiguousarray(restart)}


def kernel(**inputs):
    import concourse.bacc as bacc
    from concourse.bass_utils import run_bass_kernel_spmd

    nc = bacc.Bacc("TRN2", target_bir_lowering=False, num_devices=1)
    given = dict(inputs)
    ctx = inputs["ctx_1024"].transpose(0, 2, 1)
    rem = np.tile(ctx[:, :, KMAIN:], (1, 1, HALF - 1))
    pad = np.zeros((B, D, CTX_COLS - KMAIN - KEYS - rem.shape[2]), ctx.dtype)
    given["ctx_1024"] = np.concatenate([ctx[:, :, :KMAIN], ctx, rem, pad], axis=2)
    given["x"] = inputs["x"].transpose(1, 0, 2)
    given["L0_ffn_expert_sel"] = inputs["L0_ffn_expert_sel"].T
    given["L0_ffn_keys"] = inputs["L0_ffn_keys"].transpose(1, 0, 2).reshape(D, EXPERTS * FE)
    given["L0_ffn_values"] = inputs["L0_ffn_values"].reshape(BLOCKS, P, D).transpose(1, 0, 2).reshape(P, BLOCKS * D)
    arrays = {f"in_{n}": np.ascontiguousarray(given[n]) for n in _INS} | shape_constants()
    args = [nc.dram_tensor(n, a.shape, mybir.dt.from_np(a.dtype), kind="ExternalInput").ap() for n, a in arrays.items()]
    out = nc.dram_tensor("out_0", (B, S, D), F32, kind="ExternalOutput").ap()
    gates_dram = nc.dram_tensor("gates_dram", (EXPERTS, GT), F32, kind="Internal").ap()
    build(nc, *args, out, gates_dram)
    result = run_bass_kernel_spmd(nc, [arrays], core_ids=[0])
    return result.results[0]["out_0"]
```
